# Optimizing a Trainium2 kernel written in Bass

```python
import numpy as np
import jax
import jax.numpy as jnp

def _softmax(x, axis=-1):
    return jax.nn.softmax(x, axis=axis)

def _gelu(x):
    return jax.nn.gelu(x, approximate=True)

def _silu(x):
    return jax.nn.silu(x)

def _sigmoid(x):
    return jax.nn.sigmoid(x)

def _layernorm(x, axis=-1, eps=1e-05):
    m = jnp.mean(x, axis=axis, keepdims=True)
    v = jnp.var(x, axis=axis, keepdims=True)
    return (x - m) / jnp.sqrt(v + eps)

def _scatter_add(tgt, idx, src, axis=0):
    return tgt.at[idx].add(src)

def _segment_sum(src, seg, n):
    return jax.ops.segment_sum(src, seg, n)
kernel_name = 'mk_vit_tower_d4_tok_img256_r4_aff801'

def setup_inputs(seed: int=0):
    np.random.seed(seed)
    _w = jnp.asarray

    def _rec_inputs():
        import jax
        import jax.numpy as jnp
        _rk = jax.random.key(seed)
        x = -7.10856e-05 + 0.999911 * jax.random.normal(jax.random.fold_in(_rk, 1), (8, 64, 128, 64), jnp.float32)
        return x
    x = _rec_inputs()

    def _L0_tok_setup():
        import jax, jax.numpy as jnp
        import numpy as np
        PATCH_LEN = 16
        STRIDE = 8
        PAD = 8
        key = jax.random.key(seed)
        k1, k2 = jax.random.split(key)
        x = jax.random.normal(k1, (32, 64, 128, 64), dtype=jnp.float32)
        in_feat = 64 * (PATCH_LEN // 2 + 1) * 2
        W = jax.random.normal(k2, (64, in_feat), dtype=jnp.float32) * 0.02
        return {'x': x, 'W': W}
    _L0_tok_all = _L0_tok_setup()
    _L0_tok_in = {k: v for k, v in _L0_tok_all.items() if k in ('W',)}
    del _L0_tok_all

    def _L0_attn_setup():
        import jax, jax.numpy as jnp
        import numpy as np
        import math
        B, T, D = (4, 256, 64)
        H = 4
        DH = D // H
        SHIFTS = (0, 4, 8, 12)
        WINDOW = 64
        key = jax.random.key(seed)
        ks = jax.random.split(key, 9)
        sc = 1.0 / math.sqrt(D)
        return {'x': jax.random.normal(ks[0], (B, T, D), jnp.float32), 'Wq': jax.random.normal(ks[1], (D, D), jnp.float32) * sc, 'bq': jnp.zeros((D,), jnp.float32), 'Wk': jax.random.normal(ks[2], (D, D), jnp.float32) * sc, 'bk': jnp.zeros((D,), jnp.float32), 'Wv': jax.random.normal(ks[3], (D, D), jnp.float32) * sc, 'bv': jnp.zeros((D,), jnp.float32), 'Wo': jax.random.normal(ks[4], (D, D), jnp.float32) * sc, 'bo': jnp.zeros((D,), jnp.float32), 'shift_logits': jnp.zeros((H, len(SHIFTS)), jnp.float32), 'alibi_slope': jnp.ones((H,), jnp.float32) * 0.01}
    _L0_attn_all = _L0_attn_setup()
    _L0_attn_in = {k: v for k, v in _L0_attn_all.items() if k in ('Wq', 'bq', 'Wk', 'bk', 'Wv', 'bv', 'Wo', 'bo', 'shift_logits', 'alibi_slope')}
    del _L0_attn_all

    def _L0_ffn_setup():
        import jax, jax.numpy as jnp
        import numpy as np
        NUM_EXPERTS = 8
        TOP_K = 2
        B, S, D = (8, 2048, 64)

        def _moe(tokens, router_w, w1, b1, w2, b2):
            N = tokens.shape[0]
            E = router_w.shape[0]
            logits = tokens.astype(jnp.float32) @ router_w.astype(jnp.float32).T
            probs = jax.nn.softmax(logits, axis=-1)
            rw, re = jax.lax.top_k(probs, TOP_K)
            if TOP_K > 1:
                rw = rw / jnp.maximum(rw.sum(-1, keepdims=True), 1e-12)
            rw = rw.astype(tokens.dtype)
            combine = jnp.zeros((N, E), tokens.dtype).at[jnp.arange(N)[:, None], re].set(rw)
            out = tokens
            for e in range(E):
                h = jax.nn.gelu(tokens @ w1[e] + b1[e], approximate=False)
                y = h @ w2[e] + b2[e]
                out = out + combine[:, e:e + 1] * y
            return out
        key = jax.random.key(seed)
        ks = jax.random.split(key, 4)
        scale = 1.0 / np.sqrt(D).astype(np.float32)
        return {'input_embeddings': jax.random.normal(ks[0], (B, S, D), jnp.float32), 'router_w': jax.random.normal(ks[1], (NUM_EXPERTS, D), jnp.float32) * scale, 'w1': jax.random.normal(ks[2], (NUM_EXPERTS, D, D), jnp.float32) * scale, 'b1': jnp.zeros((NUM_EXPERTS, D), jnp.float32), 'w2': jax.random.normal(ks[3], (NUM_EXPERTS, D, D), jnp.float32) * scale, 'b2': jnp.zeros((NUM_EXPERTS, D), jnp.float32)}
    _L0_ffn_all = _L0_ffn_setup()
    _L0_ffn_in = {k: v for k, v in _L0_ffn_all.items() if k in ('router_w', 'w1', 'b1', 'w2', 'b2')}
    del _L0_ffn_all

    def _L1_attn_setup():
        import jax, jax.numpy as jnp
        import numpy as np
        NHEAD = 8
        ATT_EPS = 1e-06
        LN_EPS = 1e-05

        def _layernorm(x, g, b):
            mu = jnp.mean(x, axis=-1, keepdims=True)
            var = jnp.mean(jnp.square(x - mu), axis=-1, keepdims=True)
            return (x - mu) * jax.lax.rsqrt(var + LN_EPS) * g + b
        key = jax.random.key(seed)
        ks = jax.random.split(key, 7)
        N, L, C = (4, 4096, 64)
        s = 1.0 / np.sqrt(C)
        return {'x': jax.random.normal(ks[0], (N, L, C), jnp.float32), 'Wq': jax.random.normal(ks[1], (C, C), jnp.float32) * s, 'Wk': jax.random.normal(ks[2], (C, C), jnp.float32) * s, 'Wv': jax.random.normal(ks[3], (C, C), jnp.float32) * s, 'Wm': jax.random.normal(ks[4], (C, C), jnp.float32) * s, 'W1': jax.random.normal(ks[5], (2 * C, 2 * C), jnp.float32) * (1.0 / np.sqrt(2 * C)), 'W2': jax.random.normal(ks[6], (2 * C, C), jnp.float32) * (1.0 / np.sqrt(2 * C)), 'g1': jnp.ones((C,), jnp.float32), 'b1': jnp.zeros((C,), jnp.float32), 'g2': jnp.ones((C,), jnp.float32), 'b2': jnp.zeros((C,), jnp.float32)}
    _L1_attn_all = _L1_attn_setup()
    _L1_attn_in = {k: v for k, v in _L1_attn_all.items() if k in ('Wq', 'Wk', 'Wv', 'Wm', 'W1', 'W2', 'g1', 'b1', 'g2', 'b2')}
    del _L1_attn_all

    def _L1_ffn_setup():
        import jax, jax.numpy as jnp
        import numpy as np
        B, S, D, H, E, K = (8, 2048, 64, 256, 8, 2)
        key = jax.random.key(seed)
        ks = jax.random.split(key, 7)
        s_in = 1.0 / np.sqrt(D)
        s_hid = 1.0 / np.sqrt(H)
        return {'x': jax.random.normal(ks[0], (B, S, D), dtype=jnp.float32), 'Wg': jax.random.uniform(ks[1], (E, D), jnp.float32, -s_in, s_in), 'bg': jax.random.uniform(ks[2], (E,), jnp.float32, -s_in, s_in), 'W1': jax.random.uniform(ks[3], (E, H, D), jnp.float32, -s_in, s_in), 'b1': jax.random.uniform(ks[4], (E, H), jnp.float32, -s_in, s_in), 'W2': jax.random.uniform(ks[5], (E, D, H), jnp.float32, -s_hid, s_hid), 'b2': jax.random.uniform(ks[6], (E, D), jnp.float32, -s_hid, s_hid)}
    _L1_ffn_all = _L1_ffn_setup()
    _L1_ffn_in = {k: v for k, v in _L1_ffn_all.items() if k in ('Wg', 'bg', 'W1', 'b1', 'W2', 'b2')}
    del _L1_ffn_all

    def _L2_attn_setup():
        import jax, jax.numpy as jnp
        import numpy as np
        key = jax.random.key(seed)
        k1, k2, k3 = jax.random.split(key, 3)
        d = 64
        x = jax.random.normal(k1, (8, 512, d), dtype=jnp.float32)
        Wq = jax.random.normal(k2, (d, d), dtype=jnp.float32) * d ** (-0.5)
        Wk = jax.random.normal(k3, (d, d), dtype=jnp.float32) * d ** (-0.5)
        return {'x': x, 'Wq': Wq, 'Wk': Wk}
    _L2_attn_all = _L2_attn_setup()
    _L2_attn_in = {k: v for k, v in _L2_attn_all.items() if k in ('Wq', 'Wk')}
    del _L2_attn_all

    def _L2_ffn_setup():
        import jax, jax.numpy as jnp
        import numpy as np
        TOP_K = 2
        key = jax.random.key(seed)
        ks = jax.random.split(key, 4)
        B, L, D, H, E = (8, 1024, 64, 256, 8)
        s = 0.02
        return {'x': jax.random.normal(ks[0], (B, L, D), jnp.float32), 'Wg': jax.random.normal(ks[1], (D, E), jnp.float32) * s, 'bg': jnp.zeros((E,), jnp.float32), 'W1': jax.random.normal(ks[2], (E, D, H), jnp.float32) * s, 'b1': jnp.zeros((E, H), jnp.float32), 'W2': jax.random.normal(ks[3], (E, H, D), jnp.float32) * s, 'b2': jnp.zeros((E, D), jnp.float32)}
    _L2_ffn_all = _L2_ffn_setup()
    _L2_ffn_in = {k: v for k, v in _L2_ffn_all.items() if k in ('Wg', 'bg', 'W1', 'b1', 'W2', 'b2')}
    del _L2_ffn_all

    def _L3_attn_setup():
        import jax, jax.numpy as jnp
        import numpy as np
        B, T, C, HR = (8, 1024, 64, 4)
        N_LAYER, LAYER_ID = (12, 3)
        HID = HR * C

        def _fancy_decay_first():
            r01 = LAYER_ID / (N_LAYER - 1)
            h = np.arange(C, dtype=np.float32)
            decay = -5.0 + 8.0 * (h / (C - 1)) ** (0.7 + 1.3 * r01)
            zig = (np.arange(1, C + 1) % 3 - 1).astype(np.float32) * 0.5
            first = np.float32(np.log(0.3)) + zig
            return (jnp.asarray(decay, jnp.float32), jnp.asarray(first, jnp.float32))

        def _ln(x, g, b):
            m = jnp.mean(x, axis=-1, keepdims=True)
            v = jnp.var(x, axis=-1, keepdims=True)
            return (x - m) * jax.lax.rsqrt(v + 1e-05) * g + b

        def _wkv(w, u, k, v):
            Bb, Tt, Cc = k.shape
            kT = jnp.swapaxes(k, 0, 1)
            vT = jnp.swapaxes(v, 0, 1)

            def step(carry, kv):
                p, q, o = carry
                kt, vt = kv
                no = jnp.maximum(o, u + kt)
                A = jnp.exp(o - no)
                E = jnp.exp(u + kt - no)
                y = (A * p + E * vt) / (A * q + E)
                no2 = jnp.maximum(w + o, kt)
                A2 = jnp.exp(w + o - no2)
                E2 = jnp.exp(kt - no2)
                return ((A2 * p + E2 * vt, A2 * q + E2, no2), y)
            init = (jnp.zeros((Bb, Cc), k.dtype), jnp.zeros((Bb, Cc), k.dtype), jnp.full((Bb, Cc), -1e+38, k.dtype))
            _, yT = jax.lax.scan(step, init, (kT, vT))
            return jnp.swapaxes(yT, 0, 1)
        key = jax.random.key(seed)
        ks = jax.random.split(key, 12)
        s = 0.02
        decay, first = _fancy_decay_first()
        return {'x': jax.random.normal(ks[0], (B, T, C), jnp.float32), 'Wk': jax.random.normal(ks[1], (C, C), jnp.float32) * s, 'Wv': jax.random.normal(ks[2], (C, C), jnp.float32) * s, 'Wr': jax.random.normal(ks[3], (C, C), jnp.float32) * s, 'Wo': jax.random.normal(ks[4], (C, C), jnp.float32) * s, 'Wk_ffn': jax.random.normal(ks[5], (C, HID), jnp.float32) * s, 'Wv_ffn': jax.random.normal(ks[6], (HID, C), jnp.float32) * s, 'Wr_ffn': jax.random.normal(ks[7], (C, C), jnp.float32) * s, 'g1': 1.0 + 0.1 * jax.random.normal(ks[8], (C,), jnp.float32), 'b1': 0.1 * jax.random.normal(ks[9], (C,), jnp.float32), 'g2': 1.0 + 0.1 * jax.random.normal(ks[10], (C,), jnp.float32), 'b2': 0.1 * jax.random.normal(ks[11], (C,), jnp.float32), 'spatial_decay': decay, 'spatial_first': first}
    _L3_attn_all = _L3_attn_setup()
    _L3_attn_in = {k: v for k, v in _L3_attn_all.items() if k in ('Wk', 'Wv', 'Wr', 'Wo', 'Wk_ffn', 'Wv_ffn', 'Wr_ffn', 'g1', 'b1', 'g2', 'b2', 'spatial_decay', 'spatial_first')}
    del _L3_attn_all

    def _L3_ffn_setup():
        import jax, jax.numpy as jnp
        import numpy as np
        C = 64
        HID = 256
        E = 8
        TEMP = 1.0
        key = jax.random.key(seed)
        ks = jax.random.split(key, 7)
        x = jax.random.normal(ks[0], (8, 4096, C), dtype=jnp.float32)
        W1 = jax.random.normal(ks[1], (C, HID), dtype=jnp.float32) * 0.02
        b1 = jnp.zeros((HID,), dtype=jnp.float32)
        Wg = jax.random.normal(ks[2], (HID, E), dtype=jnp.float32) * 0.02
        bg = jnp.zeros((E,), dtype=jnp.float32)
        Wd = jax.random.normal(ks[3], (E, HID, C), dtype=jnp.float32) * 0.02
        bd = jnp.zeros((E, C), dtype=jnp.float32)
        return {'x': x, 'W1': W1, 'b1': b1, 'Wg': Wg, 'bg': bg, 'Wd': Wd, 'bd': bd}
    _L3_ffn_all = _L3_ffn_setup()
    _L3_ffn_in = {k: v for k, v in _L3_ffn_all.items() if k in ('W1', 'b1', 'Wg', 'bg', 'Wd', 'bd')}
    del _L3_ffn_all
    return {'x': x, 'L0_tok_W': _L0_tok_in['W'], 'L0_attn_Wq': _L0_attn_in['Wq'], 'L0_attn_bq': _L0_attn_in['bq'], 'L0_attn_Wk': _L0_attn_in['Wk'], 'L0_attn_bk': _L0_attn_in['bk'], 'L0_attn_Wv': _L0_attn_in['Wv'], 'L0_attn_bv': _L0_attn_in['bv'], 'L0_attn_Wo': _L0_attn_in['Wo'], 'L0_attn_bo': _L0_attn_in['bo'], 'L0_attn_shift_logits': _L0_attn_in['shift_logits'], 'L0_attn_alibi_slope': _L0_attn_in['alibi_slope'], 'L0_ffn_router_w': _L0_ffn_in['router_w'], 'L0_ffn_w1': _L0_ffn_in['w1'], 'L0_ffn_b1': _L0_ffn_in['b1'], 'L0_ffn_w2': _L0_ffn_in['w2'], 'L0_ffn_b2': _L0_ffn_in['b2'], 'L1_attn_Wq': _L1_attn_in['Wq'], 'L1_attn_Wk': _L1_attn_in['Wk'], 'L1_attn_Wv': _L1_attn_in['Wv'], 'L1_attn_Wm': _L1_attn_in['Wm'], 'L1_attn_W1': _L1_attn_in['W1'], 'L1_attn_W2': _L1_attn_in['W2'], 'L1_attn_g1': _L1_attn_in['g1'], 'L1_attn_b1': _L1_attn_in['b1'], 'L1_attn_g2': _L1_attn_in['g2'], 'L1_attn_b2': _L1_attn_in['b2'], 'L1_ffn_Wg': _L1_ffn_in['Wg'], 'L1_ffn_bg': _L1_ffn_in['bg'], 'L1_ffn_W1': _L1_ffn_in['W1'], 'L1_ffn_b1': _L1_ffn_in['b1'], 'L1_ffn_W2': _L1_ffn_in['W2'], 'L1_ffn_b2': _L1_ffn_in['b2'], 'L2_attn_Wq': _L2_attn_in['Wq'], 'L2_attn_Wk': _L2_attn_in['Wk'], 'L2_ffn_Wg': _L2_ffn_in['Wg'], 'L2_ffn_bg': _L2_ffn_in['bg'], 'L2_ffn_W1': _L2_ffn_in['W1'], 'L2_ffn_b1': _L2_ffn_in['b1'], 'L2_ffn_W2': _L2_ffn_in['W2'], 'L2_ffn_b2': _L2_ffn_in['b2'], 'L3_attn_Wk': _L3_attn_in['Wk'], 'L3_attn_Wv': _L3_attn_in['Wv'], 'L3_attn_Wr': _L3_attn_in['Wr'], 'L3_attn_Wo': _L3_attn_in['Wo'], 'L3_attn_Wk_ffn': _L3_attn_in['Wk_ffn'], 'L3_attn_Wv_ffn': _L3_attn_in['Wv_ffn'], 'L3_attn_Wr_ffn': _L3_attn_in['Wr_ffn'], 'L3_attn_g1': _L3_attn_in['g1'], 'L3_attn_b1': _L3_attn_in['b1'], 'L3_attn_g2': _L3_attn_in['g2'], 'L3_attn_b2': _L3_attn_in['b2'], 'L3_attn_spatial_decay': _L3_attn_in['spatial_decay'], 'L3_attn_spatial_first': _L3_attn_in['spatial_first'], 'L3_ffn_W1': _L3_ffn_in['W1'], 'L3_ffn_b1': _L3_ffn_in['b1'], 'L3_ffn_Wg': _L3_ffn_in['Wg'], 'L3_ffn_bg': _L3_ffn_in['bg'], 'L3_ffn_Wd': _L3_ffn_in['Wd'], 'L3_ffn_bd': _L3_ffn_in['bd']}

def reference(x, L0_tok_W, L0_attn_Wq, L0_attn_bq, L0_attn_Wk, L0_attn_bk, L0_attn_Wv, L0_attn_bv, L0_attn_Wo, L0_attn_bo, L0_attn_shift_logits, L0_attn_alibi_slope, L0_ffn_router_w, L0_ffn_w1, L0_ffn_b1, L0_ffn_w2, L0_ffn_b2, L1_attn_Wq, L1_attn_Wk, L1_attn_Wv, L1_attn_Wm, L1_attn_W1, L1_attn_W2, L1_attn_g1, L1_attn_b1, L1_attn_g2, L1_attn_b2, L1_ffn_Wg, L1_ffn_bg, L1_ffn_W1, L1_ffn_b1, L1_ffn_W2, L1_ffn_b2, L2_attn_Wq, L2_attn_Wk, L2_ffn_Wg, L2_ffn_bg, L2_ffn_W1, L2_ffn_b1, L2_ffn_W2, L2_ffn_b2, L3_attn_Wk, L3_attn_Wv, L3_attn_Wr, L3_attn_Wo, L3_attn_Wk_ffn, L3_attn_Wv_ffn, L3_attn_Wr_ffn, L3_attn_g1, L3_attn_b1, L3_attn_g2, L3_attn_b2, L3_attn_spatial_decay, L3_attn_spatial_first, L3_ffn_W1, L3_ffn_b1, L3_ffn_Wg, L3_ffn_bg, L3_ffn_Wd, L3_ffn_bd):
    import jax
    import jax.numpy as jnp

    def _L0_tok_ref(x, W):
        import jax, jax.numpy as jnp
        import numpy as np
        PATCH_LEN = 16
        STRIDE = 8
        PAD = 8
        B, C, T, V = x.shape
        xp = jnp.pad(x, ((0, 0), (0, 0), (0, PAD), (0, 0)), mode='edge')
        Tp = T + PAD
        N = (Tp - PATCH_LEN) // STRIDE + 1
        idx = jnp.arange(N)[:, None] * STRIDE + jnp.arange(PATCH_LEN)[None, :]
        patches = xp[:, :, idx, :]
        patches = jnp.transpose(patches, (0, 4, 2, 3, 1))
        xf = jnp.fft.rfft(patches, axis=-2, norm='ortho')
        F = xf.shape[-2]
        x_real = xf.real.reshape(B, V, N, F * C)
        x_imag = xf.imag.reshape(B, V, N, F * C)
        x_emb = jnp.concatenate([x_real, x_imag], axis=-1)
        x_emb = x_emb @ W.T
        return x_emb.reshape(B, V * N, -1)

    def _L0_attn_ref(x, Wq, bq, Wk, bk, Wv, bv, Wo, bo, shift_logits, alibi_slope):
        import jax, jax.numpy as jnp
        import numpy as np
        import math
        B, T, D = (4, 256, 64)
        H = 4
        DH = D // H
        SHIFTS = (0, 4, 8, 12)
        WINDOW = 64
        Bt, Tt, Dd = x.shape

        def split(y):
            return y.reshape(Bt, Tt, H, DH).transpose(0, 2, 1, 3)
        q = split(x @ Wq.T + bq)
        k0 = split(x @ Wk.T + bk)
        v0 = split(x @ Wv.T + bv)

        def shift_time(t, s):
            if s == 0:
                return t
            return jnp.pad(t[:, :, :Tt - s, :], ((0, 0), (0, 0), (s, 0), (0, 0)))
        K = jnp.stack([shift_time(k0, s) for s in SHIFTS], axis=2)
        V = jnp.stack([shift_time(v0, s) for s in SHIFTS], axis=2)
        qn = q / math.sqrt(DH)
        att = jnp.einsum('bhtd,bhskd->bhstk', qn, K)
        pos = jnp.arange(Tt)
        rel = pos[None, :] - pos[:, None]
        dist = jnp.clip(rel, 0, None).astype(att.dtype)
        alibi = -alibi_slope[:, None, None] * dist
        if WINDOW is not None and WINDOW < Tt:
            keep = (rel >= 0) & (rel < WINDOW)
            mask = jnp.where(keep, 0.0, -10000.0).astype(att.dtype)
            att = att + mask[None, None, None]
        att = att + alibi[None, :, None]
        pi = jax.nn.softmax(shift_logits, axis=-1)
        att = att + jnp.log(pi + 1e-08)[None, :, :, None, None]
        att = jax.scipy.special.logsumexp(att, axis=2)
        p = jax.nn.softmax(att, axis=-1)
        ctx = jnp.einsum('bhtk,bhskd->bhtd', p, V)
        out = ctx.transpose(0, 2, 1, 3).reshape(Bt, Tt, H * DH)
        return out @ Wo.T + bo

    def _L0_ffn_ref(input_embeddings, router_w, w1, b1, w2, b2):
        import jax, jax.numpy as jnp
        import numpy as np
        NUM_EXPERTS = 8
        TOP_K = 2
        B, S, D = (8, 2048, 64)

        def _moe(tokens, router_w, w1, b1, w2, b2):
            N = tokens.shape[0]
            E = router_w.shape[0]
            logits = tokens.astype(jnp.float32) @ router_w.astype(jnp.float32).T
            probs = jax.nn.softmax(logits, axis=-1)
            rw, re = jax.lax.top_k(probs, TOP_K)
            if TOP_K > 1:
                rw = rw / jnp.maximum(rw.sum(-1, keepdims=True), 1e-12)
            rw = rw.astype(tokens.dtype)
            combine = jnp.zeros((N, E), tokens.dtype).at[jnp.arange(N)[:, None], re].set(rw)
            out = tokens
            for e in range(E):
                h = jax.nn.gelu(tokens @ w1[e] + b1[e], approximate=False)
                y = h @ w2[e] + b2[e]
                out = out + combine[:, e:e + 1] * y
            return out
        b, s, d = input_embeddings.shape
        tokens = input_embeddings.reshape(b * s, d)
        return _moe(tokens, router_w, w1, b1, w2, b2).reshape(b, s, d)

    def _L1_attn_ref(x, Wq, Wk, Wv, Wm, W1, W2, g1, b1, g2, b2):
        import jax, jax.numpy as jnp
        import numpy as np
        NHEAD = 8
        ATT_EPS = 1e-06
        LN_EPS = 1e-05

        def _layernorm(x, g, b):
            mu = jnp.mean(x, axis=-1, keepdims=True)
            var = jnp.mean(jnp.square(x - mu), axis=-1, keepdims=True)
            return (x - mu) * jax.lax.rsqrt(var + LN_EPS) * g + b
        N, L, C = x.shape
        H = NHEAD
        D = C // H
        q = (x @ Wq).reshape(N, L, H, D)
        k = (x @ Wk).reshape(N, L, H, D)
        v = (x @ Wv).reshape(N, L, H, D)
        Q = jax.nn.elu(q) + 1.0
        K = jax.nn.elu(k) + 1.0
        v = v / L
        KV = jnp.einsum('nshd,nshv->nhdv', K, v)
        Z = 1.0 / (jnp.einsum('nlhd,nhd->nlh', Q, K.sum(axis=1)) + ATT_EPS)
        msg = jnp.einsum('nlhd,nhdv,nlh->nlhv', Q, KV, Z) * L
        msg = msg.reshape(N, L, C) @ Wm
        msg = _layernorm(msg, g1, b1)
        h = jnp.concatenate([x, msg], axis=-1) @ W1
        h = jax.nn.relu(h) @ W2
        msg = _layernorm(h, g2, b2)
        return x + msg

    def _L1_ffn_ref(x, Wg, bg, W1, b1, W2, b2):
        import jax, jax.numpy as jnp
        import numpy as np
        B, S, D, H, E, K = (8, 2048, 64, 256, 8, 2)
        gate_scores = jnp.einsum('bsd,ed->bse', x, Wg) + bg
        topk_scores, topk_idx = jax.lax.top_k(gate_scores, K)
        topk_probs = jax.nn.softmax(topk_scores, axis=-1)
        combine = jnp.sum(topk_probs[..., None] * jax.nn.one_hot(topk_idx, E, dtype=x.dtype), axis=-2)
        out = jnp.zeros_like(x)
        for e in range(E):
            h = jax.nn.relu(jnp.einsum('bsd,hd->bsh', x, W1[e]) + b1[e])
            y = jnp.einsum('bsh,dh->bsd', h, W2[e]) + b2[e]
            out = out + combine[..., e:e + 1] * y
        return out

    def _L2_attn_ref(x, Wq, Wk):
        import jax, jax.numpy as jnp
        import numpy as np
        d = x.shape[-1]
        scale = d ** (-0.5)
        q = jnp.einsum('bnd,ed->bne', x, Wq)
        k = jnp.einsum('bnd,ed->bne', x, Wk)
        sim = jnp.einsum('bid,bjd->bij', q, k) * scale
        attn = jax.nn.softmax(sim, axis=-1)
        out = jnp.einsum('bij,bjd->bid', attn, x)
        return out

    def _L2_ffn_ref(x, Wg, bg, W1, b1, W2, b2):
        import jax, jax.numpy as jnp
        import numpy as np
        TOP_K = 2
        B, L, D = x.shape
        E = W1.shape[0]
        xf = x.reshape(-1, D)
        gate_logits = xf @ Wg + bg
        top_w, top_i = jax.lax.top_k(gate_logits, TOP_K)
        top_w = jax.nn.softmax(top_w, axis=-1)
        w_dense = jnp.sum(jax.nn.one_hot(top_i, E, dtype=xf.dtype) * top_w[..., None], axis=1)
        out = jnp.zeros_like(xf)
        for e in range(E):
            h = jax.nn.gelu(xf @ W1[e] + b1[e], approximate=False)
            out = out + w_dense[:, e:e + 1] * (h @ W2[e] + b2[e])
        return out.reshape(B, L, D)

    def _L3_attn_ref(x, Wk, Wv, Wr, Wo, Wk_ffn, Wv_ffn, Wr_ffn, g1, b1, g2, b2, spatial_decay, spatial_first):
        import jax, jax.numpy as jnp
        import numpy as np
        B, T, C, HR = (8, 1024, 64, 4)
        N_LAYER, LAYER_ID = (12, 3)
        HID = HR * C

        def _fancy_decay_first():
            r01 = LAYER_ID / (N_LAYER - 1)
            h = np.arange(C, dtype=np.float32)
            decay = -5.0 + 8.0 * (h / (C - 1)) ** (0.7 + 1.3 * r01)
            zig = (np.arange(1, C + 1) % 3 - 1).astype(np.float32) * 0.5
            first = np.float32(np.log(0.3)) + zig
            return (jnp.asarray(decay, jnp.float32), jnp.asarray(first, jnp.float32))

        def _ln(x, g, b):
            m = jnp.mean(x, axis=-1, keepdims=True)
            v = jnp.var(x, axis=-1, keepdims=True)
            return (x - m) * jax.lax.rsqrt(v + 1e-05) * g + b

        def _wkv(w, u, k, v):
            Bb, Tt, Cc = k.shape
            kT = jnp.swapaxes(k, 0, 1)
            vT = jnp.swapaxes(v, 0, 1)

            def step(carry, kv):
                p, q, o = carry
                kt, vt = kv
                no = jnp.maximum(o, u + kt)
                A = jnp.exp(o - no)
                E = jnp.exp(u + kt - no)
                y = (A * p + E * vt) / (A * q + E)
                no2 = jnp.maximum(w + o, kt)
                A2 = jnp.exp(w + o - no2)
                E2 = jnp.exp(kt - no2)
                return ((A2 * p + E2 * vt, A2 * q + E2, no2), y)
            init = (jnp.zeros((Bb, Cc), k.dtype), jnp.zeros((Bb, Cc), k.dtype), jnp.full((Bb, Cc), -1e+38, k.dtype))
            _, yT = jax.lax.scan(step, init, (kT, vT))
            return jnp.swapaxes(yT, 0, 1)
        Tlen = x.shape[1]
        h = _ln(x, g1, b1)
        k = h @ Wk
        v = h @ Wv
        sr = jax.nn.sigmoid(h @ Wr)
        y = _wkv(spatial_decay / Tlen, spatial_first / Tlen, k, v)
        x = x + sr * y @ Wo
        h2 = _ln(x, g2, b2)
        kk = jnp.square(jax.nn.relu(h2 @ Wk_ffn))
        x = x + jax.nn.sigmoid(h2 @ Wr_ffn) * (kk @ Wv_ffn)
        return x

    def _L3_ffn_ref(x, W1, b1, Wg, bg, Wd, bd):
        import jax, jax.numpy as jnp
        import numpy as np
        C = 64
        HID = 256
        E = 8
        TEMP = 1.0
        orig_shape = x.shape
        xf = x.reshape(-1, orig_shape[-1])
        H = jax.nn.gelu(xf @ W1 + b1, approximate=False)
        probs = jax.nn.softmax((H @ Wg + bg) / TEMP, axis=-1)
        assign = jnp.argmax(probs, axis=-1)
        out = jnp.zeros_like(xf)
        for e in range(Wd.shape[0]):
            y = H @ Wd[e] + bd[e]
            sel = (assign == e)[:, None]
            out = out + jnp.where(sel, probs[:, e:e + 1] * y, 0.0)
        return out.reshape(orig_shape)
    h = _L0_tok_ref(x, L0_tok_W)
    h = h + _L0_attn_ref(_layernorm(h, axis=-1), L0_attn_Wq, L0_attn_bq, L0_attn_Wk, L0_attn_bk, L0_attn_Wv, L0_attn_bv, L0_attn_Wo, L0_attn_bo, L0_attn_shift_logits, L0_attn_alibi_slope)
    h = h + _L0_ffn_ref(_layernorm(h, axis=-1), L0_ffn_router_w, L0_ffn_w1, L0_ffn_b1, L0_ffn_w2, L0_ffn_b2)
    h = h + _L1_attn_ref(_layernorm(h, axis=-1), L1_attn_Wq, L1_attn_Wk, L1_attn_Wv, L1_attn_Wm, L1_attn_W1, L1_attn_W2, L1_attn_g1, L1_attn_b1, L1_attn_g2, L1_attn_b2)
    h = h + _L1_ffn_ref(_layernorm(h, axis=-1), L1_ffn_Wg, L1_ffn_bg, L1_ffn_W1, L1_ffn_b1, L1_ffn_W2, L1_ffn_b2)
    h = h + _L2_attn_ref(_layernorm(h, axis=-1), L2_attn_Wq, L2_attn_Wk)
    h = h + _L2_ffn_ref(_layernorm(h, axis=-1), L2_ffn_Wg, L2_ffn_bg, L2_ffn_W1, L2_ffn_b1, L2_ffn_W2, L2_ffn_b2)
    h = h + _L3_attn_ref(_layernorm(h, axis=-1), L3_attn_Wk, L3_attn_Wv, L3_attn_Wr, L3_attn_Wo, L3_attn_Wk_ffn, L3_attn_Wv_ffn, L3_attn_Wr_ffn, L3_attn_g1, L3_attn_b1, L3_attn_g2, L3_attn_b2, L3_attn_spatial_decay, L3_attn_spatial_first)
    h = h + _L3_ffn_ref(_layernorm(h, axis=-1), L3_ffn_W1, L3_ffn_b1, L3_ffn_Wg, L3_ffn_bg, L3_ffn_Wd, L3_ffn_bd)
    return h

_drawn_inputs = setup_inputs


def setup_inputs(seed=0):
    import zlib

    import numpy as np

    out = dict(_drawn_inputs(seed))
    spreads = {'L0_attn_bq': (0.0, 0.1),
     'L0_attn_bk': (0.0, 0.8),
     'L0_attn_bv': (0.0, 0.1),
     'L0_attn_bo': (0.0, 0.1),
     'L0_attn_shift_logits': (0.0, 0.425),
     'L0_attn_alibi_slope': (0.009999999776482582, 0.2),
     'L0_ffn_b1': (0.0, 0.271),
     'L0_ffn_b2': (0.0, 0.1),
     'L1_attn_g1': (1.0, 0.2),
     'L1_attn_b1': (0.0, 0.1),
     'L1_attn_g2': (1.0, 0.2),
     'L1_attn_b2': (0.0, 0.1),
     'L2_ffn_bg': (0.0, 0.412),
     'L2_ffn_b1': (0.0, 0.8),
     'L2_ffn_b2': (0.0, 0.345),
     'L3_ffn_b1': (0.0, 2.0),
     'L3_ffn_bg': (0.0, 2.0),
     'L3_ffn_bd': (0.0, 2.0)}
    factors = {'L1_attn_Wq': 3.691,
     'L1_ffn_bg': 3.836,
     'L1_ffn_b1': 8.0,
     'L1_ffn_b2': 6.515,
     'L2_ffn_Wg': 3.389,
     'L2_ffn_W1': 8.0,
     'L2_ffn_W2': 8.0,
     'L3_attn_Wk': 8.0,
     'L3_attn_Wv': 8.0,
     'L3_attn_Wr': 8.0,
     'L3_attn_Wo': 8.0,
     'L3_attn_Wk_ffn': 8.0,
     'L3_attn_Wv_ffn': 8.0,
     'L3_attn_Wr_ffn': 8.0,
     'L3_attn_g1': 8.0,
     'L3_attn_b1': 8.0,
     'L3_attn_g2': 8.0,
     'L3_attn_b2': 8.0,
     'L3_attn_spatial_decay': 8.0,
     'L3_attn_spatial_first': 64.0,
     'L3_ffn_W1': 64.0,
     'L3_ffn_Wg': 64.0,
     'L3_ffn_Wd': 64.0}
    for name, (base, spread) in spreads.items():
        noise = np.random.default_rng([zlib.crc32(name.encode()), seed]).standard_normal(out[name].shape)
        drawn = base * np.exp(spread * noise) if base else spread * noise
        out[name] = jnp.asarray(drawn.astype(out[name].dtype))
    for name, factor in factors.items():
        out[name] = (out[name] * factor).astype(out[name].dtype)
    return out
```

```python
import numpy as np
import concourse.bass as bass
from concourse import mybir
from contextlib import ExitStack

F32 = mybir.dt.float32
U32 = mybir.dt.uint32
ALU = mybir.AluOpType
ACT = mybir.ActivationFunctionType
AX = mybir.AxisListType.X

B = 8
C = 64
T_IN = 128
V = 64
PATCH, STRIDE = 16, 8
NP = T_IN // STRIDE
L = V * NP
TT = L // 128
NF = PATCH // 2 + 1
E = 8
HID = 256
EPS = 1e-5
HALF = L // 2

H0, DH0 = 4, 16
SHIFTS = (0, 4, 8, 12)
SMAX = SHIFTS[-1]
WINDOW = 64
QB = 32
NQ = L // QB
KW = 96
SW = KW + SMAX
LP = SMAX + L + WINDOW
MASKED = -30000.0

H1, D1 = 8, 8
ATT_EPS = 1e-6

IMAGES = {
    "tok": [("wt", NF * C), ("dft", NF * NF), ("sel_first", 192), ("sel_second", 192)],
    "attn0": [("wq", 128), ("wk", 128), ("wv", C), ("wo", C), ("bq", 1), ("bk", 1), ("slope", 1), ("shift", 4),
              ("svals", 4), ("dist", SW), ("pen", SW), ("headmask", C), ("selq", QB), ("keep", 128),
              ("right", WINDOW)],
    "moe0": [("w1", E * C), ("w2", 4 * 128), ("wr", E), ("b1", 4), ("b2", E * C)],
    "attn1": [("wq", C), ("wkv", 2 * C), ("wm", C), ("w1", 128), ("w2", C), ("g1", C), ("b1", C),
              ("g2", C), ("b2", C), ("head", C), ("zero", C)],
    "moe1": [("w1", E * HID), ("w2", 16 * C), ("wr", E), ("b1", 16), ("b2", E * C), ("br", E)],
    "attn2": [("wqk", 256)],
    "moe2": [("w1", E * HID), ("w2", 16 * C), ("wr", E), ("b1", 16), ("b2", E * C), ("br", E)],
    "attn3": [("wk", 128), ("wv", 128), ("wr", 128), ("wo", 128), ("wkf", 4 * 128), ("wvf", 4 * 128), ("wrf", 128),
              ("g1", 1), ("b1", 1), ("g2", 1), ("b2", 1), ("decay", 1), ("first", 1)],
    "moe3": [("w1", HID), ("b1", 2), ("wr", 2 * E), ("w2", 2 * E * C), ("b2", E * C), ("br", E)],
}


def columns(image):
    at, out = 0, {}
    for name, n in IMAGES[image]:
        out[name] = (at, n)
        at += n
    return out, at


class Memory:

    def __init__(self, nc, ctx):
        self.nc, self.ctx = nc, ctx
        self.h = self.sb("h", [128, B, TT, C])
        self.ident = self.sb("ident", [128, 128])
        self.halves = self.sb("halves", [128, TT])
        self.eps = self.sb("eps", [128, TT])
        self.carrier = self.sb("carrier", [128, 1])
        self.iota = self.sb("iota", [128, TT, E])
        self.xn = self.sb("xn", [128, TT, C])
        self.xc = self.sb("xc", [128, TT, C])
        self.bs = self.sb("bs", [128, TT, 6])
        self.mv = self.sb("mv", [128, 6, TT])
        self.ve = self.sb("ve", [128, TT])
        self.rs = self.sb("rs", [128, TT])
        self.pairs = [ctx.enter_context(nc.psum_tensor(f"banks{k}", [128, 1024], F32)) for k in range(4)]
        self.bank = [self.pairs[k // 2][:, 512 * (k % 2):512 * (k % 2) + 512] for k in range(8)]

    def sb(self, name, shape, dt=F32):
        return self.ctx.enter_context(self.nc.sbuf_tensor(name, shape, dt))


def per_tile(stat, width=C):
    return stat.unsqueeze(2).to_broadcast([128, TT, width])


ORDER = (0, 2, 4, 6, 1, 3, 5, 7)

LN_STEPS = 14


def layernorm_vector(nc, dve, mem, m, sems, before_write=None):
    normalise(nc, dve, mem, lambda t: mem.h[:, m, t, :], mem.h[:, m, :, :], mem.xn[:], m, sems, before_write)


def normalise(nc, dve, mem, tile, src, out, m, sems, before_write=None):
    base, steps = m * LN_STEPS, sems["ln_steps"]
    for t in range(TT):
        nc.vector.bn_stats(mem.bs[:, t, :], tile(t)).then_inc(steps, 1)
    dve.wait_ge(steps, base + 8)
    bs = mem.bs
    nc.vector.tensor_tensor(mem.mv[:, 0], bs[:, :, 1], bs[:, :, 4], ALU.add).then_inc(steps, 1)
    nc.vector.tensor_tensor(mem.mv[:, 1], bs[:, :, 1], bs[:, :, 4], ALU.subtract).then_inc(steps, 1)
    nc.vector.tensor_tensor(mem.mv[:, 2], bs[:, :, 2], bs[:, :, 5], ALU.add).then_inc(steps, 1)
    dve.wait_ge(steps, base + 11)
    nc.vector.tensor_scalar(mem.mv[:, 3], mem.mv[:, 0], 0.5, None, ALU.mult).then_inc(steps, 1)
    nc.vector.scalar_tensor_tensor(mem.mv[:, 4], mem.mv[:, 1], 0.25, mem.mv[:, 1], ALU.mult, ALU.mult
                                   ).then_inc(steps, 1)
    dve.wait_ge(steps, base + 13)
    nc.vector.scalar_tensor_tensor(mem.mv[:, 5], mem.mv[:, 2], 1.0 / C, mem.mv[:, 4], ALU.mult, ALU.add
                                   ).then_inc(sems["stats_ready"], 1)
    nc.vector.tensor_tensor(mem.xc[:], src, per_tile(mem.mv[:, 3]), ALU.subtract).then_inc(steps, 1)
    dve.wait_ge(steps, base + 14)
    dve.wait_ge(sems["rstd_ready"], m + 1)
    if before_write:
        before_write()
    nc.vector.tensor_tensor(out, mem.xc[:], per_tile(mem.rs[:]), ALU.mult).then_inc(sems["xn_ready"], 1)


def layernorm_pool(nc, pool, mem, m, sems):
    pool.wait_ge(sems["stats_ready"], m + 1)
    nc.gpsimd.tensor_tensor(mem.ve[:], mem.mv[:, 5], mem.eps[:], ALU.add).then_inc(sems["ve_ready"], 1)
    pool.wait_ge(sems["ve_ready"], m + 1)
    nc.gpsimd.tensor_tensor(mem.rs[:], mem.ve[:], mem.halves[:], ALU.pow).then_inc(sems["rstd_ready"], 1)


LN_SEMS = ("ln_steps", "stats_ready", "ve_ready", "rstd_ready", "xn_ready")


def wait_past(eng, sem, count):
    if not (isinstance(count, int) and count <= 0):
        eng.wait_ge(sem, count)


def first_then_loop(eng, rounds, each):
    each(0)
    with eng.Fori(1, rounds) as i:
        each(i)


def carry_wait(nc, mem):
    nc.vector.tensor_copy(mem.carrier[:], mem.eps[:, 0:1])


def open_sems(nc, ctx, stage, names):
    sems = {n: nc.alloc_semaphore(f"{stage}_{n}") for n in names}

    def close():
        nc.clear_and_free_semaphores(list(sems.values()))
        nc.all_engine_barrier()

    ctx.callback(close)
    return sems


def load_image(nc, ctx, mem, stage, images):
    at, width = columns(stage)
    w = mem.images[stage]
    return lambda name, rows=slice(0, 128): w[rows, at[name][0]:at[name][0] + at[name][1]]


def stage_tok(nc, mem, x, images):
    with ExitStack() as ctx:
        sb = lambda n, s: ctx.enter_context(nc.sbuf_tensor(n, s, F32))
        raw = sb("raw", [128, 2, 8, STRIDE, V])
        x1 = sb("x1", [128, STRIDE, 8, V])
        x2 = sb("x2", [128, STRIDE, 8, V])
        edge_x = sb("edge_x", [C, 2, V])
        cs = sb("cs", [128, NF, C])
        we = sb("we", [128, STRIDE, C])
        wo = sb("wo", [128, STRIDE, C])
        S = open_sems(nc, ctx, "tok", ("img", "xa", "xb", "ea", "eb", "fold", "fold_psum", "folded", "copied_lo",
                                       "copied_hi", "tokens", "kept", "other"))
        w = load_image(nc, ctx, mem, "tok", images)
        wt = w("wt").rearrange("p (f d) -> p f d", d=C)
        dft = w("dft")
        loaded, edge = (S["xa"], S["xb"]), (S["ea"], S["eb"])
        xr = x.rearrange("b c (s two j) v -> b c s two (j v)", two=2, j=STRIDE)
        late = [n for n in IMAGES if n != "tok"]
        block = ctx.enter_context(nc.Block())

        def load_x(sp, b, par):
            for half in range(2):
                sp.dma_start(raw[64 * half:64 * half + 64, par].rearrange("c s j v -> c s (j v)"),
                             xr[b, :, :, half, :]).then_inc(loaded[par], 16)
            sp.dma_start(edge_x[:, par, :], x[b, :, T_IN - 1, :]).then_inc(edge[par], 16)

        @block.sync
        def _(sp):
            sp.dma_start(mem.images["tok"][:], images["tok"]).then_inc(S["img"], 16)
            for par in range(2):
                load_x(sp, par, par)
            with sp.Fori(1, B // 2) as i:
                for par in range(2):
                    sp.wait_ge(S["copied_lo"], 2 * (2 * i - 1 + par))
                    sp.wait_ge(S["copied_hi"], 2 * (2 * i - 1 + par))
                    load_x(sp, 2 * i + par, par)
            for n in late:
                sp.dma_start(mem.images[n][:], images[n]).then_inc(S["other"], 16)
            sp.dma_start(mem.ident[:], images["ident"]).then_inc(S["other"], 16)
            sp.dma_start(mem.iota[:].rearrange("p t e -> p (t e)"), images["iota"]).then_inc(S["other"], 16)
            sp.wait_ge(S["other"], 16 * (len(late) + 2))

        @block.gpsimd
        def _(pool):
            nc.gpsimd.memset(mem.halves[:], -0.5)
            nc.gpsimd.memset(mem.eps[:], EPS)

        @block.vector
        def _(dve):
            dve.wait_ge(S["img"], 16)
            nc.vector.memset(cs[:], 0.0).then_inc(S["fold"], 1)
            for f in range(NF):
                for j in range(NF):
                    n = 1 + f * NF + j
                    dve.wait_ge(S["fold"], max(1, n - NF + 1))
                    nc.vector.scalar_tensor_tensor(cs[:, j, :], wt[:, f, :], dft[:, f * NF + j:f * NF + j + 1],
                                                   cs[:, j, :], ALU.mult, ALU.add).then_inc(S["fold"], 1)
            dve.wait_ge(S["fold_psum"], 1)
            nc.vector.tensor_copy(we[:].rearrange("p j d -> p (j d)"), mem.bank[0][:]).then_inc(S["folded"], 1)
            nc.vector.tensor_copy(wo[:].rearrange("p j d -> p (j d)"), mem.bank[1][:]).then_inc(S["folded"], 1)
            def each(i):
                for par in range(2):
                    dve.wait_ge(loaded[par], 32 * i + 32)
                    wait_past(dve, S["tokens"], 2 * i + par)
                    nc.vector.tensor_copy(x1[:].rearrange("c j s v -> c s j v"), raw[:, par]
                                          ).then_inc(S["copied_hi"], 1)
                    nc.vector.tensor_copy(x2[64:128].rearrange("c j s v -> c s j v"), raw[64:128, par]
                                          ).then_inc(S["copied_hi"], 1)
            first_then_loop(dve, B // 2, each)

        @block.tensor
        def _(pe):
            pe.wait_ge(S["fold"], 1 + NF * NF)
            for bank, shift in ((0, 0), (1, 64)):
                first = w("sel_first")[:, shift:shift + 128]
                second = w("sel_second")[:, shift:shift + 128]
                for j in range(STRIDE):
                    out = mem.bank[bank][:, j * C:(j + 1) * C]
                    nc.tensor.matmul(out, first, cs[:, j, :], start=True, stop=False)
                    last = nc.tensor.matmul(out, second, cs[:, STRIDE - j, :], start=False, stop=True)
            last.then_inc(S["fold_psum"], 1)
            pe.wait_ge(S["folded"], 2)
            def each(i):
                for par in range(2):
                    wait_past(pe, S["kept"], 2 * i)
                    for odd in range(2):
                        pe.wait_ge(S["copied_hi"], 4 * i + 2 * par + 1 + odd)
                        if odd:
                            pe.wait_ge(S["copied_lo"], 4 * i + 2 * par + 2)
                        src, wgt = (x2, wo) if odd else (x1, we)
                        for k in range(4):
                            u = 2 * k + odd
                            for j in range(STRIDE):
                                last = nc.tensor.matmul(
                                    mem.bank[2 + par][:, u * C:(u + 1) * C],
                                    src[:, j, 2 * k:2 * k + 2, :].rearrange("c s v -> c (s v)"),
                                    wgt[:, j, :], start=(j == 0), stop=(j == STRIDE - 1))
                    last.then_inc(S["tokens"], 1)
            first_then_loop(pe, B // 2, each)

        @block.scalar
        def _(act):
            def each(i):
                for par in range(2):
                    act.wait_ge(loaded[par], 32 * i + 32)
                    act.wait_ge(edge[par], 16 * i + 16)
                    wait_past(act, S["tokens"], 2 * i + par)
                    nc.scalar.activation(x2[0:64, :, 0:7, :].rearrange("c j s v -> c s j v"),
                                         raw[0:64, par, 1:8, :, :], ACT.Copy).then_inc(S["copied_lo"], 1)
                    nc.scalar.activation(x2[0:64, :, 7, :],
                                         edge_x[:, par, :].unsqueeze(1).to_broadcast([C, STRIDE, V]), ACT.Copy
                                         ).then_inc(S["copied_lo"], 1)
                    act.wait_ge(S["tokens"], 2 * i + par + 1)
                    nc.scalar.activation(mem.h[:, 2 * i + par, :, :].rearrange("p t c -> p (t c)"),
                                         mem.bank[2 + par][:], ACT.Copy).then_inc(S["kept"], 1)
            first_then_loop(act, B // 2, each)


def stage_moe(nc, mem, stage, images):
    shared, top2, residual, relu = stage == "moe3", stage != "moe3", stage == "moe0", stage == "moe1"
    chunks = {"moe0": 4, "moe1": 16, "moe2": 16, "moe3": 2}[stage]
    with ExitStack() as ctx:
        sb = lambda n, s, d=F32: ctx.enter_context(nc.sbuf_tensor(f"{stage}_{n}", s, d))
        w = load_image(nc, ctx, mem, stage, images)
        w1, b1, wr, w2 = w("w1"), w("b1"), w("wr"), w("w2")
        xt = sb("xt", [128, L], FR)
        w1h, w1l = sb("w1h", [128, 128 * chunks], FR), sb("w1l", [128, 128 * chunks], FR)
        wrh, wrl = sb("wrh", [128, E], FR), sb("wrl", [128, E], FR)
        hid = sb("hid", [128, 2, chunks, HALF])
        lg = sb("lg", [128, TT, E])
        m8 = sb("m8", [128, TT, 8])
        i8 = sb("i8", [128, TT, 8], U32)
        dif = sb("dif", [128, TT])
        ex = sb("ex", [128, TT, E])
        wtop = sb("wtop", [128, 2, TT])
        hot = sb("hot", [128, 2, TT, E])
        cw = sb("cw", [128, TT, E])
        cwt = sb("cwt", [C, 128])
        b2d = sb("b2d", [C, TT, C])
        prod = sb("prod", [128, 2, 512])
        res = sb("res", [128, TT, C])
        S = open_sems(nc, ctx, stage, LN_SEMS + XT_SEMS + (
            "wsplit", "b2_zero", "b2_loaded", "scored", "gate", "picked", "exp_ready", "weights_ready",
            "hidden", "hid_ready", "experts", "experts_used", "summed", "cwt_psum", "cwt_ready", "bias_psum",
            "comb", "h_plus_xn"))
        TB, SC, BB = (mem.bank[0], mem.bank[1]), mem.bank[2], mem.bank[3]
        HB, YB = (mem.bank[4], mem.bank[5]), (mem.bank[6], mem.bank[7])
        NH = 2 * chunks
        block = ctx.enter_context(nc.Block())

        @block.sync
        def _(sp):
            sp.wait_ge(S["b2_zero"], 1)
            at = columns(stage)[0]["b2"][0]
            for t in range(TT):
                sp.dma_start(b2d[E * t:E * t + E, t, :], images[stage][0:E, at:at + C]).then_inc(S["b2_loaded"], 16)
            sp.wait_ge(S["b2_loaded"], 16 * TT)

        @block.gpsimd
        def _(pool):
            nc.gpsimd.memset(b2d[:], 0.0).then_inc(S["b2_zero"], 1)
            def each(m):
                layernorm_pool(nc, pool, mem, m, S)
            first_then_loop(pool, B, each)

        GATE = 9 if top2 else 5

        def gate(dve, i):
            base = i * GATE
            k = [0]

            def step(ins):
                k[0] += 1
                ins.then_inc(S["gate"], 1)

            def own():
                dve.wait_ge(S["gate"], base + k[0])

            dve.wait_ge(S["scored"], i + 1)
            scores = SC[:, 0:TT * E].rearrange("p (t e) -> p t e", e=E)
            if stage == "moe0":
                step(nc.vector.tensor_copy(lg[:], scores))
            else:
                step(nc.vector.tensor_tensor(lg[:], scores, w("br").unsqueeze(1).to_broadcast([128, TT, E]), ALU.add))
            own()
            carry_wait(nc, mem)
            for t in range(TT):
                ins = nc.vector.max(m8[:, t, :], lg[:, t, :])
            step(ins)
            own()
            carry_wait(nc, mem)
            for t in range(TT):
                ins = nc.vector.max_index(i8[:, t, :], m8[:, t, :], lg[:, t, :])
            step(ins)
            own()
            if top2:
                nc.vector.tensor_tensor(dif[:], m8[:, :, 0], m8[:, :, 1], ALU.subtract).then_inc(S["picked"], 1)
                for n in range(2):
                    step(nc.vector.tensor_tensor(hot[:, n], mem.iota[:], per_tile(i8[:, :, n], E), ALU.is_equal))
                dve.wait_ge(S["exp_ready"], i + 1)
                step(nc.vector.tensor_scalar(wtop[:, 0], ex[:, :, 0], 0.5, 0.5, ALU.mult, ALU.add))
                step(nc.vector.tensor_scalar(wtop[:, 1], ex[:, :, 0], -0.5, 0.5, ALU.mult, ALU.add))
                own()
                for n in range(2):
                    step(nc.vector.tensor_tensor(hot[:, n], hot[:, n], per_tile(wtop[:, n], E), ALU.mult))
                own()
                assert k[0] == GATE
                wait_past(dve, S["cwt_psum"], i)
                nc.vector.tensor_tensor(cw[:], hot[:, 0], hot[:, 1], ALU.add).then_inc(S["weights_ready"], 1)
            else:
                nc.vector.tensor_tensor(lg[:], lg[:], per_tile(m8[:, :, 0], E), ALU.subtract).then_inc(S["picked"], 1)
                nc.vector.tensor_tensor(hot[:, 0], mem.iota[:], per_tile(i8[:, :, 0], E), ALU.is_equal)
                dve.wait_ge(S["exp_ready"], i + 1)
                step(nc.vector.tensor_reduce(dif[:], ex[:], AX, ALU.add))
                own()
                step(nc.vector.reciprocal(wtop[:, 0], dif[:]))
                own()
                assert k[0] == GATE
                wait_past(dve, S["cwt_psum"], i)
                nc.vector.tensor_tensor(cw[:], hot[:, 0], per_tile(wtop[:, 0], E), ALU.mult
                                        ).then_inc(S["weights_ready"], 1)

        def combine(dve, i, g):
            dve.wait_ge(S["weights_ready"], i + 1)
            for n in range(4):
                t = 4 * g + n
                u = 2 * n + g
                dve.wait_ge(S["experts"], i * TT + t + 1)
                wait_past(dve, S["summed"], i * TT + (t - 1 if t >= 2 else 0))
                y = YB[t % 2].rearrange("p (e d) -> p e d", d=C)
                out = prod[:, t % 2, :].rearrange("p (e d) -> p e d", d=C)
                nc.vector.tensor_tensor(out, y, cw[:, u, :].unsqueeze(2).to_broadcast([128, E, C]), ALU.mult
                                        ).then_inc(S["experts_used"], 1)
                dve.wait_ge(S["experts_used"], i * TT + t + 1)
                nc.vector.tensor_reduce(res[:, u, :], prod[:, t % 2, :].rearrange("p (e d) -> p d e", d=C),
                                        AX, ALU.add).then_inc(S["summed"], 1)

        def keep(dve, i):
            dve.wait_ge(S["summed"], i * TT + TT)
            dve.wait_ge(S["bias_psum"], i + 1)
            nc.vector.tensor_tensor(res[:], res[:], BB.rearrange("p (t c) -> p t c", c=C), ALU.add
                                    ).then_inc(S["comb"], 1)
            dve.wait_ge(S["comb"], 2 * i + 1)
            if residual:
                dve.wait_ge(S["h_plus_xn"], i + 1)
            nc.vector.tensor_tensor(mem.h[:, i, :, :], mem.h[:, i, :, :], res[:], ALU.add).then_inc(S["comb"], 1)

        def norm(dve, m):
            layernorm_vector(nc, dve, mem, m, S, lambda: wait_past(dve, S["turned"], m))
            if residual:
                dve.wait_ge(S["xn_ready"], m + 1)
                nc.vector.tensor_tensor(mem.h[:, m, :, :], mem.h[:, m, :, :], mem.xn[:], ALU.add
                                        ).then_inc(S["h_plus_xn"], 1)

        @block.vector
        def _(dve):
            split_weight(nc, dve, w1, w1h[:], w1l[:], S["wsplit"], 0)
            if not shared:
                split_weight(nc, dve, wr, wrh[:], wrl[:], S["wsplit"], 2)
            norm(dve, 0)
            spread_vector(nc, dve, 0, S, TB, xt, in_tiles)
            if not shared:
                gate(dve, 0)

            def body(i, last):
                if shared:
                    gate(dve, i)
                if not last:
                    norm(dve, i + 1)
                combine(dve, i, 0)
                if not last:
                    dve.wait_ge(S["hidden"], (i + 1) * NH)
                    spread_vector(nc, dve, i + 1, S, TB, xt, in_tiles)
                combine(dve, i, 1)
                if not last and not shared:
                    gate(dve, i + 1)
                keep(dve, i)

            def each(i):
                body(i, False)
            first_then_loop(dve, B - 1, each)
            body(B - 1, True)

        @block.scalar
        def _(act):
            def pick(i):
                act.wait_ge(S["picked"], i + 1)
                if top2:
                    nc.scalar.activation(ex[:, :, 0], dif[:], ACT.Tanh, scale=0.5).then_inc(S["exp_ready"], 1)
                else:
                    nc.scalar.activation(ex[:], lg[:], ACT.Exp).then_inc(S["exp_ready"], 1)

            def hidden(i, g):
                for c in range(chunks):
                    n = g * chunks + c
                    act.wait_ge(S["hidden"], i * NH + n + 1)
                    nc.scalar.activation(hid[:, g, c, :], HB[n % 2], ACT.Relu if relu else ACT.Gelu,
                                         bias=b1[:, c:c + 1]).then_inc(S["hid_ready"], 1)

            def body(i, last):
                wait_past(act, S["experts"], i * TT)
                hidden(i, 1)
                if shared:
                    pick(i)
                if not last:
                    spread_scalar(nc, act, i + 1, S, TB, xt, in_tiles)
                act.wait_ge(S["cwt_psum"], i + 1)
                nc.scalar.activation(cwt[:], SC[0:C, 128:256], ACT.Copy).then_inc(S["cwt_ready"], 1)
                if not last:
                    act.wait_ge(S["experts"], i * TT + 4)
                    hidden(i + 1, 0)
                    if not shared:
                        pick(i + 1)

            spread_scalar(nc, act, 0, S, TB, xt, in_tiles)
            hidden(0, 0)
            if not shared:
                pick(0)
            def each(i):
                body(i, False)
            first_then_loop(act, B - 1, each)
            body(B - 1, True)

        @block.tensor
        def _(pe):
            def at(t):
                return 512 * (t % 2) + 128 * (t // 2)

            def score(i):
                wait_past(pe, S["weights_ready"], i)
                wait_past(pe, S["cwt_ready"], i)
                if shared:
                    pe.wait_ge(S["hid_ready"], i * NH + NH)
                for t in range(TT):
                    out = SC[:, t * E:(t + 1) * E]
                    if shared:
                        for c in range(chunks):
                            last = nc.tensor.matmul(out, hid[:, t % 2, c, 128 * (t // 2):128 * (t // 2) + 128],
                                                    wr[:, c * E:(c + 1) * E], start=(c == 0), stop=(c == chunks - 1))
                    else:
                        tok = xt[:, at(t):at(t) + 128]
                        nc.tensor.matmul(out, tok, wrh[:], start=True, stop=False)
                        last = nc.tensor.matmul(out, tok, wrl[:], start=False, stop=True)
                last.then_inc(S["scored"], 1)

            def hidden(i, g, c0, c1):
                for c in range(c0, c1):
                    n = g * chunks + c
                    if n >= 2 or g:
                        wait_past(pe, S["hid_ready"], i * NH + n - 1)
                    elif not isinstance(i, int):
                        wait_past(pe, S["hid_ready"], i * NH + n - 1)
                    src = xt[:, 512 * g:512 * g + 512]
                    nc.tensor.matmul(HB[n % 2], w1h[:, 128 * c:128 * c + 128], src, start=True, stop=False)
                    nc.tensor.matmul(HB[n % 2], w1l[:, 128 * c:128 * c + 128], src, start=False, stop=True
                                     ).then_inc(S["hidden"], 1)

            def experts(i, g, n):
                t = 4 * g + n
                wait_past(pe, S["experts_used"], i * TT + (t - 1 if t >= 2 else 0))
                Y = YB[t % 2]
                for c in range(chunks):
                    hk = hid[:, g, c, 128 * n:128 * n + 128]
                    if stage == "moe0":
                        last = nc.tensor.matmul(Y[:, 128 * c:128 * c + 128], hk, w2[:, 128 * c:128 * c + 128],
                                                start=True, stop=True)
                    elif shared:
                        last = nc.tensor.matmul(Y, hk, w2[:, 512 * c:512 * c + 512],
                                                start=(c == 0), stop=(c == chunks - 1))
                    else:
                        e = c // 2
                        last = nc.tensor.matmul(Y[:, e * C:(e + 1) * C], hk, w2[:, c * C:(c + 1) * C],
                                                start=(c % 2 == 0), stop=(c % 2 == 1))
                last.then_inc(S["experts"], 1)

            cut = [0, chunks // 4, chunks // 2, chunks - chunks // 4, chunks] if chunks >= 4 else [0, 1, 2, 2, 2]

            def body(i, last_batch):
                pe.wait_ge(S["hid_ready"], i * NH + chunks)
                if shared:
                    hidden(i, 1, 0, chunks)
                    score(i)
                for n in range(4):
                    if not shared:
                        hidden(i, 1, cut[n], cut[n + 1])
                    if n == 3 and not last_batch:
                        turn_tensor(nc, pe, mem, i + 1, S, TB)
                    experts(i, 0, n)
                pe.wait_ge(S["weights_ready"], i + 1)
                nc.tensor.matmul(SC[0:C, 128:256], cw[:].rearrange("p t e -> p (t e)"), mem.ident[:],
                                 start=True, stop=True).then_inc(S["cwt_psum"], 1)
                pe.wait_ge(S["hid_ready"], i * NH + NH)
                experts(i, 1, 0)
                if not last_batch:
                    pe.wait_ge(S["xl_ready"], 2 * i + 4)
                    hidden(i + 1, 0, 0, cut[2])
                experts(i, 1, 1)
                if not last_batch:
                    hidden(i + 1, 0, cut[2], cut[4])
                experts(i, 1, 2)
                if not last_batch and not shared:
                    score(i + 1)
                experts(i, 1, 3)
                pe.wait_ge(S["cwt_ready"], i + 1)
                wait_past(pe, S["comb"], 2 * i)
                nc.tensor.matmul(BB, cwt[:], b2d[:].rearrange("c t d -> c (t d)"), start=True, stop=True
                                 ).then_inc(S["bias_psum"], 1)

            pe.wait_ge(S["wsplit"], 2 if shared else 4)
            pe.wait_ge(S["b2_loaded"], 16 * TT)
            turn_tensor(nc, pe, mem, 0, S, TB)
            pe.wait_ge(S["xl_ready"], 2)
            hidden(0, 0, 0, chunks)
            if not shared:
                score(0)
            def each(i):
                body(i, False)
            first_then_loop(pe, B - 1, each)
            body(B - 1, True)




FR = mybir.dt.float32r


def split_weight(nc, dve, src, hi, lo, sem, before):
    nc.vector.tensor_copy(hi, src).then_inc(sem, 1)
    dve.wait_ge(sem, before + 1)
    nc.vector.tensor_tensor(lo, src, hi.bitcast(F32), ALU.subtract).then_inc(sem, 1)


def turn_tensor(nc, pe, mem, i, S, banks, src=None):
    pe.wait_ge(S["xn_ready"], i + 1)
    wait_past(pe, S["xl_ready"], 2 * i)
    for k in range(4):
        for r in range(2):
            out, tok = banks[r][0:C, 128 * k:128 * k + 128], mem.xn[:, 2 * k + r, :]
            if k == r == 0:
                nc.tensor.matmul(out, tok, mem.ident[:], start=True, stop=True)
            else:
                last = nc.tensor.transpose(out, tok, mem.ident[:])
    last.then_inc(S["turned"], 1)


def in_tiles(xt, rows, r):
    return xt[rows, 512 * r:512 * r + 512]


def in_tokens(xt, rows, r):
    return xt[rows, 0:L].rearrange("c (v m two) -> c two m v", m=8, two=2)[:, r]


def bank_mv(bank):
    return bank.rearrange("c (m v) -> c m v", m=8)


def spread_scalar(nc, act, i, S, banks, xt, order):
    act.wait_ge(S["turned"], i + 1)
    for r in range(2):
        src = banks[r][0:C, :] if order is in_tiles else bank_mv(banks[r][0:C, :])
        nc.scalar.activation(order(xt, slice(0, C), r), src, ACT.Copy).then_inc(S["xh_ready"], 1)


def spread_vector(nc, dve, i, S, banks, xt, order):
    for r in range(2):
        dve.wait_ge(S["xh_ready"], 2 * i + r + 1)
        src = banks[r][0:C, :] if order is in_tiles else bank_mv(banks[r][0:C, :])
        nc.vector.tensor_tensor(order(xt, slice(C, 128), r), src, order(xt, slice(0, C), r).bitcast(F32),
                                ALU.subtract).then_inc(S["xl_ready"], 1)


XT_SEMS = ("turned", "xh_ready", "xl_ready")


def stage_attn2(nc, mem, stage, images):
    with ExitStack() as ctx:
        sb = lambda n, s, d=F32: ctx.enter_context(nc.sbuf_tensor(f"{stage}_{n}", s, d))
        xt = sb("xt", [128, L], FR)
        wh, wl = sb("wh", [128, 256], FR), sb("wl", [128, 256], FR)
        qs = sb("qs", [128, L], FR)
        kh, kl = sb("kh", [128, L], FR), sb("kl", [128, L], FR)
        top = sb("top", [128, TT])
        ssum = sb("ssum", [128, TT])
        rsum = sb("rsum", [128, TT])
        p = sb("p", [128, 2, L])
        pt = sb("pt", [128, 2, L])
        S = open_sems(nc, ctx, stage, LN_SEMS + XT_SEMS + (
            "wsplit", "proj", "q_hi", "qk_lo", "scored", "topped", "exped", "p_turned", "pt_ready", "mixed",
            "recip", "added"))
        w = load_image(nc, ctx, mem, stage, images)
        TQ = (mem.bank[0], mem.bank[1])
        SC = ((mem.bank[2], mem.bank[3]), (mem.bank[4], mem.bank[5]))
        PT = (mem.bank[6], mem.bank[7])
        pair = {0: mem.pairs[1], 1: mem.pairs[2]}
        block = ctx.enter_context(nc.Block())

        @block.gpsimd
        def _(pool):
            def each(m):
                layernorm_pool(nc, pool, mem, m, S)
            first_then_loop(pool, B, each)

        @block.vector
        def _(dve):
            nc.vector.tensor_scalar(w("wqk")[:, 0:128], w("wqk")[:, 0:128], C ** -0.5, None, ALU.mult
                                    ).then_inc(S["wsplit"], 1)
            dve.wait_ge(S["wsplit"], 1)
            split_weight(nc, dve, w("wqk"), wh[:], wl[:], S["wsplit"], 1)
            def each(i):
                layernorm_vector(nc, dve, mem, i, S, lambda: wait_past(dve, S["mixed"], i * TT))
                wait_past(dve, S["scored"], i * TT)
                spread_vector(nc, dve, i, S, TQ, xt, in_tiles)
                for n in range(4):
                    half = n % 2
                    cols = slice(512 * half, 512 * half + 512)
                    dve.wait_ge(S["q_hi"], 4 * i + n + 1)
                    if n < 2:
                        nc.vector.tensor_tensor(qs[C:128, cols], TQ[half][C:128, :], qs[C:128, cols].bitcast(F32),
                                                ALU.subtract).then_inc(S["qk_lo"], 1)
                    else:
                        nc.vector.tensor_tensor(kl[:, cols], TQ[half][:], kh[:, cols].bitcast(F32),
                                                ALU.subtract).then_inc(S["qk_lo"], 1)

                def finish(u):
                    dve.wait_ge(S["mixed"], i * TT + u + 1)
                    dve.wait_ge(S["recip"], i * TT + u + 1)
                    nc.vector.scalar_tensor_tensor(mem.h[:, i, u, :], TQ[u % 2][:, 0:C],
                                                   rsum[:, u:u + 1], mem.h[:, i, u, :], ALU.mult, ALU.add
                                                   ).then_inc(S["added"], 1)

                def copy_pt(u):
                    dve.wait_ge(S["p_turned"], 2 * (i * TT + u) + 2)
                    nc.vector.tensor_copy(pt[:, u % 2, 512:1024], PT[1][:]).then_inc(S["pt_ready"], 1)
                    nc.vector.reciprocal(rsum[:, u:u + 1], ssum[:, u:u + 1]).then_inc(S["recip"], 1)

                for u in range(TT):
                    dve.wait_ge(S["scored"], i * TT + u + 1)
                    nc.vector.tensor_reduce(top[:, u:u + 1], pair[u % 2][:], AX, ALU.max, negate=True
                                            ).then_inc(S["topped"], 1)
                    if u >= 1:
                        copy_pt(u - 1)
                    if u >= 2:
                        finish(u - 2)
                copy_pt(TT - 1)
                finish(TT - 2)
                finish(TT - 1)
            first_then_loop(dve, B, each)

        @block.scalar
        def _(act):
            def each(i):
                wait_past(act, S["scored"], i * TT)
                spread_scalar(nc, act, i, S, TQ, xt, in_tiles)
                for n in range(4):
                    half = n % 2
                    cols = slice(512 * half, 512 * half + 512)
                    act.wait_ge(S["proj"], 4 * i + n + 1)
                    nc.scalar.activation((qs if n < 2 else kh)[:, cols], TQ[half][:], ACT.Copy
                                         ).then_inc(S["q_hi"], 1)

                def copy_pt(u):
                    act.wait_ge(S["p_turned"], 2 * (i * TT + u) + 1)
                    nc.scalar.activation(pt[:, u % 2, 0:512], PT[0][:], ACT.Copy).then_inc(S["pt_ready"], 1)

                for u in range(TT):
                    act.wait_ge(S["topped"], i * TT + u + 1)
                    if u >= 2:
                        act.wait_ge(S["p_turned"], 2 * (i * TT + u - 1))
                    nc.scalar.activation(p[:, u % 2, :], pair[u % 2][:], ACT.Exp, bias=top[:, u:u + 1],
                                         accum_out=ssum[:, u:u + 1]).then_inc(S["exped"], 1)
                    if u >= 1:
                        copy_pt(u - 1)
                copy_pt(TT - 1)
            first_then_loop(act, B, each)

        @block.tensor
        def _(pe):
            pe.wait_ge(S["wsplit"], 3)
            def each(i):
                wait_past(pe, S["added"], i * TT)
                turn_tensor(nc, pe, mem, i, S, TQ)
                pe.wait_ge(S["xl_ready"], 2 * i + 2)
                for n in range(4):
                    half = n % 2
                    if n >= 2:
                        wait_past(pe, S["qk_lo"], 4 * i + n - 1)
                    cols = slice(512 * half, 512 * half + 512)
                    wc = slice(128 * (n // 2), 128 * (n // 2) + 128)
                    nc.tensor.matmul(TQ[half][:], wh[:, wc], xt[:, cols], start=True, stop=False)
                    nc.tensor.matmul(TQ[half][:], wl[:, wc], xt[:, cols], start=False, stop=True
                                     ).then_inc(S["proj"], 1)
                pe.wait_ge(S["qk_lo"], 4 * i + 4)

                def score(u):
                    wait_past(pe, S["exped"], i * TT + (u - 1 if u >= 2 else 0))
                    at = 512 * (u % 2) + 128 * (u // 2)
                    q = qs[:, at:at + 128]
                    for half in range(2):
                        cols = slice(512 * half, 512 * half + 512)
                        out = SC[u % 2][half][:]
                        nc.tensor.matmul(out, q, kh[:, cols], start=True, stop=False)
                        last = nc.tensor.matmul(out, q, kl[:, cols], start=False, stop=True)
                    last.then_inc(S["scored"], 1)

                def turn_p(u):
                    pe.wait_ge(S["exped"], i * TT + u + 1)
                    if u >= 1:
                        pe.wait_ge(S["pt_ready"], 2 * (i * TT + u))
                    for half in range(2):
                        for c in range(4):
                            last = nc.tensor.transpose(PT[half][:, 128 * c:128 * c + 128],
                                                       p[:, u % 2, 512 * half + 128 * c:512 * half + 128 * c + 128],
                                                       mem.ident[:])
                        last.then_inc(S["p_turned"], 1)

                def mix(u):
                    pe.wait_ge(S["pt_ready"], 2 * (i * TT + u) + 2)
                    if u >= 2:
                        wait_past(pe, S["added"], i * TT + u - 1)
                    for c in range(TT):
                        last = nc.tensor.matmul(TQ[u % 2][:, 0:C], pt[:, u % 2, 128 * c:128 * c + 128],
                                                mem.xn[:, 2 * (c % 4) + c // 4, :], start=(c == 0), stop=(c == TT - 1))
                    last.then_inc(S["mixed"], 1)

                for u in range(TT):
                    score(u)
                    if u >= 1:
                        turn_p(u - 1)
                    if u >= 2:
                        mix(u - 2)
                turn_p(TT - 1)
                mix(TT - 2)
                mix(TT - 1)
            first_then_loop(pe, B, each)


def stage_attn1(nc, mem, stage, images):
    with ExitStack() as ctx:
        sb = lambda n, s, d=F32: ctx.enter_context(nc.sbuf_tensor(f"{stage}_{n}", s, d))
        w = load_image(nc, ctx, mem, stage, images)
        xt = sb("xt", [128, L], FR)
        wqh, wql = sb("wqh", [128, C], FR), sb("wql", [128, C], FR)
        wkvh, wkvl = sb("wkvh", [128, 2 * C], FR), sb("wkvl", [128, 2 * C], FR)
        qe, qr, qf = sb("qe", [C, L]), sb("qr", [C, L]), sb("qf", [C, L])
        ke, kr = sb("ke", [128, TT, C]), sb("kr", [128, TT, C])
        kf = sb("kf", [128, TT, C])
        vs = sb("vs", [128, TT, C + 1])
        kvm = sb("kvm", [C, C + H1])
        den = sb("den", [128, TT, H1])
        num = sb("num", [128, TT, C])
        msgt = sb("msgt", [C, L])
        cat = sb("cat", [128, TT, 2 * C])
        catt = sb("catt", [128, L])
        hidden = sb("hidden", [128, L])
        mn = sb("mn", [128, TT, C])
        S = open_sems(nc, ctx, stage, LN_SEMS + XT_SEMS + (
            "ones", "wsplit", "q_psum", "q_parts", "kv_psum", "k_parts", "v_ready", "feat", "kv_sum", "kvm_ready",
            "num_psum", "msg_steps", "num_ready", "msg_turned", "msgt_ready", "merged", "affine", "cat_ready",
            "cat_turned", "catt_ready", "up", "hidden_ready", "down", "x_copied", "hsum"))
        T = (mem.bank[0], mem.bank[1])
        Q = (mem.bank[2], mem.bank[3])
        KV = (mem.bank[4], mem.bank[5])
        KS = mem.bank[6]
        N = (mem.bank[4], mem.bank[5])
        MO = mem.bank[7]
        block = ctx.enter_context(nc.Block())

        def vec(name):
            return w(name).unsqueeze(1).to_broadcast([128, TT, C])

        @block.gpsimd
        def _(pool):
            nc.gpsimd.memset(vs[:], 1.0).then_inc(S["ones"], 1)
            def each(i):
                layernorm_pool(nc, pool, mem, 3 * i, S)
                pool.wait_ge(S["xn_ready"], 3 * i + 1)
                wait_past(pool, S["cat_turned"], i)
                nc.gpsimd.tensor_tensor(cat[:, :, 0:C], mem.xn[:], vec("zero"), ALU.add).then_inc(S["x_copied"], 1)
                layernorm_pool(nc, pool, mem, 3 * i + 1, S)
                layernorm_pool(nc, pool, mem, 3 * i + 2, S)
            first_then_loop(pool, B, each)

        @block.vector
        def _(dve):
            split_weight(nc, dve, w("wq"), wqh[:], wql[:], S["wsplit"], 0)
            split_weight(nc, dve, w("wkv"), wkvh[:], wkvl[:], S["wsplit"], 2)
            def each(i):
                normalise(nc, dve, mem, lambda t: mem.h[:, i, t, :], mem.h[:, i, :, :], mem.xn[:], 3 * i, S,
                          lambda: wait_past(dve, S["x_copied"], i))
                spread_vector(nc, dve, i, S, T, xt, in_tiles)
                dve.wait_ge(S["q_parts"], 2 * i + 2)
                wait_past(dve, S["num_psum"], i)
                nc.vector.scalar_tensor_tensor(qf[:], qe[:], 1.0, qr[:], ALU.min, ALU.add).then_inc(S["feat"], 1)
                dve.wait_ge(S["k_parts"], 4 * i + 4)
                nc.vector.scalar_tensor_tensor(kf[:], ke[:], 1.0, kr[:], ALU.min, ALU.add).then_inc(S["feat"], 1)
                dve.wait_ge(S["kv_sum"], i + 1)
                nc.vector.tensor_tensor(kvm[:, 0:C], KS[0:C, 0:C], w("head", slice(0, C)), ALU.mult
                                        ).then_inc(S["kvm_ready"], 1)
                nc.vector.tensor_scalar(kvm[:, C:C + H1], w("head", slice(0, C))[:, 0:C:D1], KS[0:C, C:C + 1], None,
                                        ALU.mult).then_inc(S["kvm_ready"], 1)
                dve.wait_ge(S["num_psum"], i + 1)
                for half in range(2):
                    ins = nc.vector.tensor_scalar(den[:, 4 * half:4 * half + 4, :], N[half].rearrange(
                        "p (t c) -> p t c", c=128)[:, :, C:C + H1], ATT_EPS, None, ALU.add)
                ins.then_inc(S["msg_steps"], 1)
                dve.wait_ge(S["msg_steps"], 2 * i + 1)
                nc.vector.reciprocal(den[:], den[:]).then_inc(S["msg_steps"], 1)
                dve.wait_ge(S["msg_steps"], 2 * i + 2)
                for half in range(2):
                    for t in range(4):
                        u = 4 * half + t
                        ins = nc.vector.tensor_tensor(
                            num[:, u, :].rearrange("p (h d) -> p h d", d=D1),
                            N[half].rearrange("p (t c) -> p t c", c=128)[:, t, 0:C].rearrange("p (h d) -> p h d", d=D1),
                            den[:, u, :].unsqueeze(2).to_broadcast([128, H1, D1]), ALU.mult)
                ins.then_inc(S["num_ready"], 1)
                dve.wait_ge(S["merged"], i + 1)
                mo = MO.rearrange("p (t c) -> p t c", c=C)
                normalise(nc, dve, mem, lambda t: mo[:, t, :], mo, mn[:], 3 * i + 1, S)
                dve.wait_ge(S["xn_ready"], 3 * i + 2)
                nc.vector.tensor_tensor(mn[:], mn[:], vec("g1"), ALU.mult).then_inc(S["affine"], 1)
                dve.wait_ge(S["affine"], 3 * i + 1)
                wait_past(dve, S["cat_turned"], i)
                nc.vector.tensor_tensor(cat[:, :, C:2 * C], mn[:], vec("b1"), ALU.add).then_inc(S["cat_ready"], 1)
                dve.wait_ge(S["down"], i + 1)
                normalise(nc, dve, mem, lambda t: mo[:, t, :], mo, mn[:], 3 * i + 2, S)
                dve.wait_ge(S["xn_ready"], 3 * i + 3)
                nc.vector.tensor_tensor(mn[:], mn[:], vec("g2"), ALU.mult).then_inc(S["affine"], 1)
                hb = mem.h[:, i, :, :]
                nc.vector.tensor_tensor(hb, hb, mem.xn[:], ALU.add).then_inc(S["affine"], 1)
                dve.wait_ge(S["affine"], 3 * i + 3)
                nc.vector.tensor_tensor(mn[:], mn[:], vec("b2"), ALU.add).then_inc(S["hsum"], 1)
                dve.wait_ge(S["hsum"], 2 * i + 1)
                nc.vector.tensor_tensor(hb, hb, mn[:], ALU.add).then_inc(S["hsum"], 1)
            first_then_loop(dve, B, each)

        @block.scalar
        def _(act):
            def each(i):
                spread_scalar(nc, act, i, S, T, xt, in_tiles)
                wait_past(act, S["feat"], 2 * i)
                for half in range(2):
                    act.wait_ge(S["q_psum"], 2 * i + half + 1)
                    cols = slice(512 * half, 512 * half + 512)
                    nc.scalar.activation(qe[:, cols], Q[half][0:C, :], ACT.Exp)
                    nc.scalar.activation(qr[:, cols], Q[half][0:C, :], ACT.Relu).then_inc(S["q_parts"], 1)
                for half in range(2):
                    act.wait_ge(S["kv_psum"], 2 * i + half + 1)
                    kv = KV[half].rearrange("p (t c) -> p t c", c=2 * C)
                    four = slice(4 * half, 4 * half + 4)
                    nc.scalar.activation(ke[:, four, :], kv[:, :, 0:C], ACT.Exp).then_inc(S["k_parts"], 1)
                    nc.scalar.activation(kr[:, four, :], kv[:, :, 0:C], ACT.Relu).then_inc(S["k_parts"], 1)
                    if half == 0:
                        act.wait_ge(S["ones"], 1)
                        wait_past(act, S["kv_sum"], i)
                    nc.scalar.activation(vs[:, four, 0:C], kv[:, :, C:2 * C], ACT.Copy).then_inc(S["v_ready"], 1)
                for half in range(2):
                    act.wait_ge(S["msg_turned"], 2 * i + half + 1)
                    wait_past(act, S["merged"], i)
                    nc.scalar.activation(msgt[:, 512 * half:512 * half + 512], T[half][0:C, :], ACT.Copy
                                         ).then_inc(S["msgt_ready"], 1)
                for half in range(2):
                    act.wait_ge(S["cat_turned"], i + 1)
                    nc.scalar.activation(catt[:, 512 * half:512 * half + 512], T[half], ACT.Copy
                                         ).then_inc(S["catt_ready"], 1)
                for half in range(2):
                    act.wait_ge(S["up"], 2 * i + half + 1)
                    nc.scalar.activation(hidden[:, 512 * half:512 * half + 512], Q[half], ACT.Relu
                                         ).then_inc(S["hidden_ready"], 1)
            first_then_loop(act, B, each)

        @block.tensor
        def _(pe):
            pe.wait_ge(S["wsplit"], 4)

            def cols(half):
                return slice(512 * half, 512 * half + 512)

            def at(u):
                return 512 * (u % 2) + 128 * (u // 2)

            def each(i):
                pe.wait_ge(S["xn_ready"], 3 * i + 1)
                wait_past(pe, S["catt_ready"], 2 * i)
                for k in range(4):
                    for r in range(2):
                        out, tok = T[r][0:C, 128 * k:128 * k + 128], mem.xn[:, 2 * k + r, :]
                        if k == r == 0:
                            nc.tensor.matmul(out, tok, mem.ident[:], start=True, stop=True)
                        else:
                            last = nc.tensor.transpose(out, tok, mem.ident[:])
                last.then_inc(S["turned"], 1)
                pe.wait_ge(S["xl_ready"], 2 * i + 2)
                wait_past(pe, S["hidden_ready"], 2 * i)
                for half in range(2):
                    nc.tensor.matmul(Q[half][0:C, :], wqh[:], xt[:, cols(half)], start=True, stop=False)
                    nc.tensor.matmul(Q[half][0:C, :], wql[:], xt[:, cols(half)], start=False, stop=True
                                     ).then_inc(S["q_psum"], 1)
                wait_past(pe, S["num_ready"], i)
                for half in range(2):
                    for t in range(4):
                        a = at(4 * half + t)
                        out = KV[half][:, 128 * t:128 * t + 128]
                        nc.tensor.matmul(out, xt[:, a:a + 128], wkvh[:], start=True, stop=False)
                        last = nc.tensor.matmul(out, xt[:, a:a + 128], wkvl[:], start=False, stop=True)
                    last.then_inc(S["kv_psum"], 1)
                pe.wait_ge(S["feat"], 2 * i + 2)
                pe.wait_ge(S["v_ready"], 2 * i + 2)
                for u in range(TT):
                    last = nc.tensor.matmul(KS[0:C, 0:C + 1], kf[:, u, :], vs[:, u, :], start=(u == 0),
                                            stop=(u == TT - 1))
                last.then_inc(S["kv_sum"], 1)
                pe.wait_ge(S["kvm_ready"], 2 * i + 2)
                for u in range(TT):
                    last = nc.tensor.matmul(N[u // 4][:, 128 * (u % 4):128 * (u % 4) + C + H1], qf[:, at(u):at(u) + 128],
                                            kvm[:], start=True, stop=True)
                last.then_inc(S["num_psum"], 1)
                pe.wait_ge(S["num_ready"], i + 1)
                for half in range(2):
                    for t in range(4):
                        out, tok = T[half][0:C, 128 * t:128 * t + 128], num[:, 4 * half + t, :]
                        if half == t == 0:
                            nc.tensor.matmul(out, tok, mem.ident[:], start=True, stop=True)
                        else:
                            last = nc.tensor.transpose(out, tok, mem.ident[:])
                    last.then_inc(S["msg_turned"], 1)
                pe.wait_ge(S["msgt_ready"], 2 * i + 2)
                wait_past(pe, S["hsum"], 2 * i)
                for u in range(TT):
                    last = nc.tensor.matmul(MO[:, C * u:C * u + C], msgt[:, 128 * u:128 * u + 128], w("wm", slice(0, C)),
                                            start=True, stop=True)
                last.then_inc(S["merged"], 1)
                pe.wait_ge(S["x_copied"], i + 1)
                pe.wait_ge(S["cat_ready"], i + 1)
                for u in range(TT):
                    last = nc.tensor.transpose(T[u // 4][:, 128 * (u % 4):128 * (u % 4) + 128], cat[:, u, :],
                                               mem.ident[:])
                last.then_inc(S["cat_turned"], 1)
                for half in range(2):
                    pe.wait_ge(S["catt_ready"], 2 * i + half + 1)
                    nc.tensor.matmul(Q[half], w("w1"), catt[:, cols(half)], start=True, stop=True
                                     ).then_inc(S["up"], 1)
                pe.wait_ge(S["hidden_ready"], 2 * i + 2)
                for u in range(TT):
                    last = nc.tensor.matmul(MO[:, C * u:C * u + C], hidden[:, 128 * u:128 * u + 128], w("w2"),
                                            start=True, stop=True)
                last.then_inc(S["down"], 1)
            first_then_loop(pe, B, each)


def stage_attn0(nc, mem, stage, images):
    with ExitStack() as ctx:
        sb = lambda n, s, d=F32: ctx.enter_context(nc.sbuf_tensor(f"{stage}_{n}", s, d))
        w = load_image(nc, ctx, mem, stage, images)
        xt = sb("xt", [128, L], FR)
        xp = sb("xp", [C + 1, SMAX + L])
        xs = sb("xs", [C + 1, L + WINDOW])
        wqh, wql = sb("wqh", [128, 128], FR), sb("wql", [128, 128], FR)
        wkh, wkl = sb("wkh", [128, 128], FR), sb("wkl", [128, 128], FR)
        bq = sb("bq", [128, 1])
        nslope = sb("nslope", [128, 1])
        setup = sb("setup", [128, 4, 4])
        smax, ssum, srec = sb("smax", [128, 1]), sb("ssum", [128, 1]), sb("srec", [128, 1])
        ws = sb("ws", [128, 4])
        bias = sb("bias", [128, SW])
        qd = sb("qd", [128, NQ, H0, QB])
        kt = sb("kt", [128, LP])
        vw = sb("vw", [KW, NQ, C + 1])
        top = sb("top", [128, 2, 4])
        e = sb("e", [128, 2, 4, SW])
        p = sb("p", [128, 2, 4, KW])
        pt = sb("pt", [KW, 2, 512])
        rec = sb("rec", [128, 2, 4])
        cn = sb("cn", [128, 2, 4, C])
        ctx_t = sb("ctx_t", [C + 1, L])
        S = open_sems(nc, ctx, stage, LN_SEMS + XT_SEMS + (
            "zeroed", "setup", "setup_exp", "wsplit", "xp_ready", "shifted", "xs_ready", "qk_psum", "q_ready",
            "k_ready", "v_psum", "v_ready", "scored", "topped", "exped", "mixing", "mixed", "p_turned", "pt_ready",
            "valued", "rec_ready", "cn_ready", "ctx_psum", "ctx_ready", "out_psum", "added"))
        TB = (mem.bank[0], mem.bank[1])
        SB = (mem.bank[2], mem.bank[3])
        PB = (mem.bank[4], mem.bank[5])
        CB = (mem.bank[6], mem.bank[7])
        NG = NQ // 4
        block = ctx.enter_context(nc.Block())

        @block.gpsimd
        def _(pool):
            nc.gpsimd.memset(xp[:], 0.0).then_inc(S["zeroed"], 1)
            nc.gpsimd.memset(xs[:], 0.0).then_inc(S["zeroed"], 1)
            nc.gpsimd.memset(qd[:], 0.0).then_inc(S["zeroed"], 1)
            nc.gpsimd.memset(kt[:], 0.0).then_inc(S["zeroed"], 1)
            nc.gpsimd.memset(vw[:], 1.0).then_inc(S["zeroed"], 1)
            pool.wait_ge(S["zeroed"], 5)
            nc.gpsimd.memset(ctx_t[C:C + 1, :], 1.0).then_inc(S["zeroed"], 1)
            pool.wait_ge(S["zeroed"], 6)
            nc.gpsimd.memset(xp[C:C + 1, SMAX:], 1.0).then_inc(S["zeroed"], 1)
            for n, (part, block_at) in enumerate(((64, NQ - 2), (32, NQ - 1), (64, NQ - 1))):
                pool.wait_ge(S["zeroed"], 7 + n)
                nc.gpsimd.memset(vw[part:part + 32, block_at, C:C + 1], 0.0).then_inc(S["zeroed"], 1)
            pool.wait_ge(S["zeroed"], 10)
            def each(i):
                layernorm_pool(nc, pool, mem, i, S)
                pool.wait_ge(S["xp_ready"], 2 * i + 2)
                wait_past(pool, S["v_psum"], 4 * i)
                total = xs[:, 0:L]
                nc.gpsimd.tensor_tensor(total, xp[:, SMAX:SMAX + L], xp[:, SMAX - SHIFTS[1]:SMAX - SHIFTS[1] + L],
                                        ALU.add).then_inc(S["shifted"], 1)
                pool.wait_ge(S["shifted"], 2 * i + 1)
                nc.gpsimd.tensor_tensor(total, total, xp[:, SMAX - SHIFTS[2]:SMAX - SHIFTS[2] + L], ALU.add
                                        ).then_inc(S["shifted"], 1)
                pool.wait_ge(S["shifted"], 2 * i + 2)
                nc.gpsimd.tensor_tensor(total, total, xp[:, SMAX - SHIFTS[3]:SMAX - SHIFTS[3] + L], ALU.add
                                        ).then_inc(S["xs_ready"], 1)
            first_then_loop(pool, B, each)

        @block.vector
        def _(dve):
            split_weight(nc, dve, w("wq"), wqh[:], wql[:], S["wsplit"], 0)
            split_weight(nc, dve, w("wk"), wkh[:], wkl[:], S["wsplit"], 2)
            nc.vector.tensor_scalar(bq[:], w("bq"), DH0 ** -0.5, None, ALU.mult)
            nc.vector.tensor_scalar(nslope[:], w("slope"), -1.0, None, ALU.mult).then_inc(S["setup"], 1)
            nc.vector.tensor_reduce(smax[:], w("shift"), AX, ALU.max, negate=True).then_inc(S["setup"], 1)
            dve.wait_ge(S["setup_exp"], 1)
            nc.vector.tensor_reduce(ssum[:], setup[:, 0], AX, ALU.add).then_inc(S["setup"], 1)
            dve.wait_ge(S["setup"], 3)
            nc.vector.reciprocal(srec[:], ssum[:]).then_inc(S["setup"], 1)
            dve.wait_ge(S["setup"], 4)
            nc.vector.tensor_scalar(setup[:, 2], setup[:, 0], srec[:], 1e-8, ALU.mult, ALU.add).then_inc(S["setup"], 1)
            dve.wait_ge(S["setup"], 5)
            dve.wait_ge(S["setup_exp"], 2)
            nc.vector.tensor_tensor(ws[:], setup[:, 2], setup[:, 1], ALU.mult).then_inc(S["setup"], 1)
            nc.vector.scalar_tensor_tensor(bias[:], w("dist"), nslope[:], w("pen"), ALU.mult, ALU.add
                                           ).then_inc(S["setup"], 1)
            dve.wait_ge(S["zeroed"], 10)
            nc.vector.tensor_copy(kt[:, SMAX + L:LP], w("right")).then_inc(S["setup"], 1)
            dve.wait_ge(S["setup"], 8)
            def each(i):
                layernorm_vector(nc, dve, mem, i, S)
                spread_vector(nc, dve, i, S, TB, xt, in_tokens)

                def mix(n):
                    dve.wait_ge(S["exped"], 4 * (i * NG + n + 1))
                    wait_past(dve, S["p_turned"], i * NG + (n - 1 if n >= 2 else 0))
                    for k in range(4):
                        src = e[:, n % 2, :, SMAX - SHIFTS[k]:SMAX - SHIFTS[k] + KW]
                        if k == 0:
                            ins = nc.vector.tensor_scalar(p[:, n % 2], src, ws[:, 0:1], None, ALU.mult)
                        else:
                            dve.wait_ge(S["mixing"], 3 * (i * NG + n) + k)
                            ins = nc.vector.scalar_tensor_tensor(p[:, n % 2], src, ws[:, k:k + 1], p[:, n % 2],
                                                                 ALU.mult, ALU.add)
                        ins.then_inc(S["mixing"] if k < 3 else S["mixed"], 1)

                def keep(n):
                    dve.wait_ge(S["p_turned"], i * NG + n + 1)
                    nc.vector.tensor_tensor(pt[:, n % 2].rearrange("k (b c) -> k b c", c=128),
                                            PB[n % 2][0:KW].rearrange("k (b c) -> k b c", c=128),
                                            w("keep", slice(0, KW)).unsqueeze(1).to_broadcast([KW, 4, 128]),
                                            ALU.mult).then_inc(S["pt_ready"], 1)

                def divide(n):
                    dve.wait_ge(S["valued"], i * NG + n + 1)
                    c = CB[n % 2][:, 0:4 * (C + 1)].rearrange("p (b c) -> p b c", c=C + 1)
                    nc.vector.reciprocal(rec[:, n % 2], c[:, :, C]).then_inc(S["rec_ready"], 1)
                    dve.wait_ge(S["rec_ready"], i * NG + n + 1)
                    for k in range(4):
                        ins = nc.vector.scalar_tensor_tensor(cn[:, n % 2, k, :], c[:, k, 0:C], rec[:, n % 2, k:k + 1],
                                                             w("headmask"), ALU.mult, ALU.mult)
                    ins.then_inc(S["cn_ready"], 1)

                for n in range(NG + 3):
                    if n < NG:
                        dve.wait_ge(S["scored"], i * NG + n + 1)
                        nc.vector.tensor_reduce(top[:, n % 2], SB[n % 2][:, 0:4 * SW].rearrange(
                            "p (b c) -> p b c", c=SW), AX, ALU.max, negate=True).then_inc(S["topped"], 1)
                    if 0 <= n - 2 < NG:
                        keep(n - 2)
                    if 0 <= n - 1 < NG:
                        mix(n - 1)
                    if 0 <= n - 3 < NG:
                        divide(n - 3)
                dve.wait_ge(S["out_psum"], i + 1)
                hb = mem.h[:, i, :, :]
                nc.vector.tensor_tensor(hb, hb, CB[0].rearrange("p (t c) -> p t c", c=C), ALU.add
                                        ).then_inc(S["added"], 1)
            first_then_loop(dve, B, each)

        @block.scalar
        def _(act):
            act.wait_ge(S["setup"], 2)
            nc.scalar.activation(setup[:, 0], w("shift"), ACT.Exp, bias=smax[:]).then_inc(S["setup_exp"], 1)
            nc.scalar.activation(setup[:, 1], w("svals"), ACT.Exp, scale=nslope[:]).then_inc(S["setup_exp"], 1)
            act.wait_ge(S["zeroed"], 10)
            act.wait_ge(S["setup"], 8)
            def each(i):
                act.wait_ge(S["turned"], i + 1)
                wait_past(act, S["xs_ready"], i)
                for r in range(2):
                    nc.scalar.activation(in_tokens(xp[:, SMAX:SMAX + L], slice(0, C), r), bank_mv(TB[r][0:C, :]),
                                         ACT.Copy).then_inc(S["xp_ready"], 1)
                spread_scalar(nc, act, i, S, TB, xt, in_tokens)
                wait_past(act, S["scored"], i * NG)
                for half in range(2):
                    act.wait_ge(S["qk_psum"], 4 * i + half + 1)
                    for hd in range(H0):
                        rows = slice(32 * hd, 32 * hd + 32)
                        ins = nc.scalar.activation(
                            qd[rows, NQ // 2 * half:NQ // 2 * (half + 1), hd, :],
                            TB[half][rows, :].rearrange("c (b q) -> c b q", q=QB), ACT.Identity,
                            bias=bq[rows, :], scale=DH0 ** -0.5)
                    ins.then_inc(S["q_ready"], 1)
                for half in range(2):
                    act.wait_ge(S["qk_psum"], 4 * i + half + 3)
                    nc.scalar.activation(kt[:, SMAX + 512 * half:SMAX + 512 * half + 512], TB[half], ACT.Identity,
                                         bias=w("bk")).then_inc(S["k_ready"], 1)
                wait_past(act, S["valued"], i * NG)
                for n in range(4):
                    act.wait_ge(S["v_psum"], 4 * i + n + 1)
                    nc.scalar.activation(vw[:, 8 * n:8 * n + 8, 0:C], TB[n % 2][0:KW, :].rearrange(
                        "p (b c) -> p b c", c=C), ACT.Copy).then_inc(S["v_ready"], 1)

                def ctx_out(half):
                    act.wait_ge(S["ctx_psum"], i * NG + 4 * half + 4)
                    wait_past(act, S["out_psum"], i)
                    nc.scalar.activation(
                        ctx_t[0:C, :].rearrange("c (r m v) -> c r m v", r=2, m=8)[:, :, :, 32 * half:32 * half + 32],
                        TB[half][0:C, :].rearrange("c (v m r) -> c r m v", m=8, r=2), ACT.Copy
                    ).then_inc(S["ctx_ready"], 1)

                for n in range(NG):
                    act.wait_ge(S["topped"], i * NG + n + 1)
                    wait_past(act, S["mixed"], i * NG + (n - 1 if n >= 2 else 0))
                    for k in range(4):
                        nc.scalar.activation(e[:, n % 2, k, :], SB[n % 2][:, SW * k:SW * k + SW], ACT.Exp,
                                             bias=top[:, n % 2, k:k + 1]).then_inc(S["exped"], 1)
                ctx_out(0)
                ctx_out(1)
            first_then_loop(act, B, each)

        @block.tensor
        def _(pe):
            pe.wait_ge(S["wsplit"], 4)
            pe.wait_ge(S["setup"], 8)
            def each(i):
                wait_past(pe, S["ctx_ready"], 2 * i)
                turn_tensor(nc, pe, mem, i, S, TB)
                pe.wait_ge(S["xl_ready"], 2 * i + 2)
                for n, (hi, lo) in enumerate(((wqh, wql), (wkh, wkl))):
                    for half in range(2):
                        if n:
                            pe.wait_ge(S["q_ready"], 2 * i + half + 1)
                        cols = slice(512 * half, 512 * half + 512)
                        nc.tensor.matmul(TB[half], hi[:], xt[:, cols], start=True, stop=False)
                        nc.tensor.matmul(TB[half], lo[:], xt[:, cols], start=False, stop=True
                                         ).then_inc(S["qk_psum"], 1)
                pe.wait_ge(S["xs_ready"], i + 1)
                for n in range(4):
                    if n < 2:
                        pe.wait_ge(S["k_ready"], 2 * i + n + 1)
                    else:
                        wait_past(pe, S["v_ready"], 4 * i + n - 1)
                    for m in range(8):
                        b = 8 * n + m
                        last = nc.tensor.matmul(TB[n % 2][0:KW, C * m:C * m + C], xs[:, QB * b:QB * b + KW],
                                                w("wv", slice(0, C + 1)), start=True, stop=True)
                    last.then_inc(S["v_psum"], 1)
                pe.wait_ge(S["v_ready"], 4 * i + 4)
                wait_past(pe, S["added"], i)

                def score(n):
                    wait_past(pe, S["exped"], 4 * (i * NG + (n - 1 if n >= 2 else 0)))
                    nc.tensor.matmul(SB[n % 2][:, 0:4 * SW], mem.ident[:],
                                     bias[:].unsqueeze(1).to_broadcast([128, 4, SW]), start=True, stop=False)
                    for k in range(4):
                        b = 4 * n + k
                        last = nc.tensor.matmul(SB[n % 2][:, SW * k:SW * k + SW],
                                                qd[:, b].rearrange("p h q -> p (h q)"), kt[:, QB * b:QB * b + SW],
                                                start=False, stop=(k == 3))
                    last.then_inc(S["scored"], 1)

                def turn(n):
                    pe.wait_ge(S["mixed"], i * NG + n + 1)
                    wait_past(pe, S["pt_ready"], i * NG + (n - 1 if n >= 2 else 0))
                    for k in range(4):
                        last = nc.tensor.transpose(PB[n % 2][0:KW, 128 * k:128 * k + 128], p[:, n % 2, k, :],
                                                   mem.ident[:])
                    last.then_inc(S["p_turned"], 1)

                def value(n):
                    pe.wait_ge(S["pt_ready"], i * NG + n + 1)
                    wait_past(pe, S["cn_ready"], i * NG + (n - 1 if n >= 2 else 0))
                    for k in range(4):
                        last = nc.tensor.matmul(CB[n % 2][:, (C + 1) * k:(C + 1) * k + C + 1],
                                                pt[:, n % 2, 128 * k:128 * k + 128], vw[:, 4 * n + k, :],
                                                start=True, stop=True)
                    last.then_inc(S["valued"], 1)

                def gather(n):
                    pe.wait_ge(S["cn_ready"], i * NG + n + 1)
                    for k in range(4):
                        at = 128 * (n % 4) + QB * k
                        last = nc.tensor.matmul(TB[n // 4][0:C, at:at + QB], cn[:, n % 2, k, :], w("selq"),
                                                start=True, stop=True)
                    last.then_inc(S["ctx_psum"], 1)

                for n in range(NG + 3):
                    if n < NG:
                        score(n)
                    if 0 <= n - 1 < NG:
                        turn(n - 1)
                    if 0 <= n - 2 < NG:
                        value(n - 2)
                    if 0 <= n - 3 < NG:
                        gather(n - 3)
                pe.wait_ge(S["ctx_ready"], 2 * i + 2)
                for u in range(TT):
                    at = 512 * (u % 2) + 128 * (u // 2)
                    last = nc.tensor.matmul(CB[0][:, C * u:C * u + C], ctx_t[:, at:at + 128], w("wo", slice(0, C + 1)),
                                            start=True, stop=True)
                last.then_inc(S["out_psum"], 1)
            first_then_loop(pe, B, each)



def stage_attn3(nc, mem, stage, images):
    with ExitStack() as ctx:
        sb = lambda n, s, d=F32: ctx.enter_context(nc.sbuf_tensor(f"{stage}_{n}", s, d))
        w = load_image(nc, ctx, mem, stage, images)
        x0 = sb("x0", [128, TT, 2, C])
        z = sb("z", [128, TT, 2, C])
        x1 = sb("x1", [128, TT, 2, C])
        ht = sb("ht", [128, L])
        row = {n: sb(n, [128, L]) for n in ("uk", "a2", "e2", "top", "a1", "e1", "ev", "num", "den", "sr", "sy",
                                            "wrow", "aq")}
        o, p, q = sb("o", [128, L + 1]), sb("p", [128, L + 1]), sb("q", [128, L + 1])
        wu = sb("wu", [128, 2])
        relu = sb("relu", [128, 2, HALF])
        kk = sb("kk", [128, 4, L])
        th = sb("th", [128, L])
        S = open_sems(nc, ctx, stage, LN_SEMS + (
            "consts", "turned", "ht_ready", "kvr", "uk_ready", "sr_ready", "wkv", "logs", "exps", "sy_ready",
            "x1_psum", "x1_ready", "turned2", "h2_ready", "up", "relu_ready", "kk_ready", "down", "gate_psum",
            "th_ready", "kept"))
        P0, P1, P2, P3 = mem.pairs
        block = ctx.enter_context(nc.Block())

        def tiles_of(t):
            return t.rearrange("p (u c) -> p u c", c=128)

        @block.gpsimd
        def _(pool):
            def each(j):
                for n in range(6):
                    layernorm_pool(nc, pool, mem, 6 * j + n, S)
            first_then_loop(pool, B // 2, each)

        @block.vector
        def _(dve):
            nc.vector.memset(o[:, 0:1], -1e38)
            nc.vector.memset(p[:, 0:1], 0.0)
            nc.vector.memset(q[:, 0:1], 0.0)
            nc.vector.tensor_scalar(wu[:, 0:1], w("decay"), 1.0 / L, None, ALU.mult)
            nc.vector.tensor_scalar(wu[:, 1:2], w("first"), 1.0 / L, None, ALU.mult).then_inc(S["consts"], 1)
            dve.wait_ge(S["consts"], 1)
            nc.vector.tensor_copy(row["wrow"][:], wu[:, 0:1].to_broadcast([128, L])).then_inc(S["consts"], 1)
            dve.wait_ge(S["consts"], 2)
            def each(j):
                for bb in range(2):
                    hb = mem.h[:, 2 * j + bb, :, :]
                    normalise(nc, dve, mem, lambda t: mem.h[:, 2 * j + bb, t, :], hb, x0[:, :, bb, :], 6 * j + bb, S)
                for bb in range(2):
                    dve.wait_ge(S["xn_ready"], 6 * j + bb + 1)
                    normalise(nc, dve, mem, lambda t: x0[:, t, bb, :], x0[:, :, bb, :], z[:, :, bb, :],
                              6 * j + 2 + bb, S, lambda: wait_past(dve, S["turned2"], j))
                WKV = 11
                done = [0]

                def step(ins):
                    done[0] += 1
                    ins.then_inc(S["wkv"], 1)

                def own(n=None):
                    dve.wait_ge(S["wkv"], j * WKV + (done[0] if n is None else n))

                before, after = slice(0, L), slice(1, L + 1)
                dve.wait_ge(S["kvr"], 3 * j + 1)
                step(nc.vector.tensor_tensor_scan(o[:, after], row["wrow"][:], P1[:], -1e38, ALU.add, ALU.max))
                own()
                nc.vector.scalar_tensor_tensor(row["a2"][:], o[:, before], wu[:, 0:1], o[:, after], ALU.add,
                                               ALU.subtract).then_inc(S["logs"], 1)
                nc.vector.tensor_tensor(row["e2"][:], P1[:], o[:, after], ALU.subtract).then_inc(S["logs"], 1)
                dve.wait_ge(S["uk_ready"], j + 1)
                step(nc.vector.tensor_tensor(row["top"][:], row["uk"][:], o[:, before], ALU.max))
                own()
                nc.vector.tensor_tensor(row["a1"][:], o[:, before], row["top"][:], ALU.subtract).then_inc(S["logs"], 1)
                nc.vector.tensor_tensor(row["e1"][:], row["uk"][:], row["top"][:], ALU.subtract).then_inc(S["logs"], 1)
                dve.wait_ge(S["exps"], 4 * j + 2)
                dve.wait_ge(S["kvr"], 3 * j + 2)
                step(nc.vector.tensor_tensor(row["ev"][:], row["e2"][:], P2[:], ALU.mult))
                step(nc.vector.tensor_tensor_scan(q[:, after], row["a2"][:], row["e2"][:], 0.0, ALU.mult, ALU.add))
                own(3)
                step(nc.vector.tensor_tensor_scan(p[:, after], row["a2"][:], row["ev"][:], 0.0, ALU.mult, ALU.add))
                dve.wait_ge(S["exps"], 4 * j + 4)
                own(4)
                step(nc.vector.tensor_tensor(row["den"][:], row["a1"][:], q[:, before], ALU.mult))
                own(5)
                step(nc.vector.tensor_tensor(row["num"][:], row["a1"][:], p[:, before], ALU.mult))
                step(nc.vector.tensor_tensor(row["ev"][:], row["e1"][:], P2[:], ALU.mult))
                own(6)
                step(nc.vector.tensor_tensor(row["den"][:], row["den"][:], row["e1"][:], ALU.add))
                own(8)
                step(nc.vector.tensor_tensor(row["num"][:], row["num"][:], row["ev"][:], ALU.add))
                own(9)
                step(nc.vector.reciprocal(row["den"][:], row["den"][:]))
                own()
                nc.vector.scalar_tensor_tensor(row["num"][:], row["num"][:], 0.5, row["den"][:], ALU.mult, ALU.mult
                                               ).then_inc(S["kept"], 1)
                dve.wait_ge(S["sr_ready"], j + 1)
                dve.wait_ge(S["kept"], 5 * j + 1)
                wait_past(dve, S["x1_psum"], j)
                ins = None
                for r in range(2):
                    ins = nc.vector.scalar_tensor_tensor(
                        bank_mv(row["sy"][:, 512 * r:512 * r + 512]), in_tokens(row["sr"], slice(0, 128), r), 1.0,
                        in_tokens(row["num"], slice(0, 128), r), ALU.add, ALU.mult)
                ins.then_inc(S["sy_ready"], 1)
                assert done[0] == WKV
                dve.wait_ge(S["x1_psum"], j + 1)
                nc.vector.tensor_tensor(x1[:].rearrange("p u b c -> p (u b c)"), x0[:].rearrange("p u b c -> p (u b c)"),
                                        P0[:], ALU.add).then_inc(S["x1_ready"], 1)
                dve.wait_ge(S["x1_ready"], j + 1)
                for bb in range(2):
                    normalise(nc, dve, mem, lambda t: x1[:, t, bb, :], x1[:, :, bb, :], z[:, :, bb, :],
                              6 * j + 4 + bb, S)
                for n in range(8):
                    dve.wait_ge(S["relu_ready"], 8 * j + n + 1)
                    bank = (P2, P3)[(n // 2) % 2][:, 512 * (n % 2):512 * (n % 2) + 512]
                    nc.vector.tensor_tensor(kk[:, n // 2, 512 * (n % 2):512 * (n % 2) + 512], bank, relu[:, n % 2, :],
                                            ALU.mult).then_inc(S["kk_ready"], 1)
                dve.wait_ge(S["down"], j + 1)
                dve.wait_ge(S["th_ready"], j + 1)
                nc.vector.scalar_tensor_tensor(row["aq"][:], th[:], 1.0, P0[:], ALU.add, ALU.mult).then_inc(S["kept"], 1)
                dve.wait_ge(S["kept"], 5 * j + 2)
                nc.vector.scalar_tensor_tensor(x1[:].rearrange("p u b c -> p (u b c)"), row["aq"][:], 0.5,
                                               x1[:].rearrange("p u b c -> p (u b c)"), ALU.mult, ALU.add
                                               ).then_inc(S["kept"], 1)
                dve.wait_ge(S["kept"], 5 * j + 3)
                for bb in range(2):
                    hb = mem.h[:, 2 * j + bb, :, :]
                    nc.vector.tensor_tensor(hb, hb, x1[:, :, bb, :], ALU.add).then_inc(S["kept"], 1)
            first_then_loop(dve, B // 2, each)

        @block.scalar
        def _(act):
            act.wait_ge(S["consts"], 1)
            def each(j):
                act.wait_ge(S["turned"], j + 1)
                for r in range(2):
                    nc.scalar.activation(in_tokens(ht, slice(0, 128), r), bank_mv(P0[:, 512 * r:512 * r + 512]),
                                         ACT.Identity, bias=w("b1"), scale=w("g1")).then_inc(S["ht_ready"], 1)
                act.wait_ge(S["kvr"], 3 * j + 1)
                wait_past(act, S["kept"], 5 * j)
                wait_past(act, S["wkv"], 11 * j)
                act.wait_ge(S["logs"], 4 * j + 2)
                nc.scalar.activation(row["uk"][:], P1[:], ACT.Identity, bias=wu[:, 1:2]).then_inc(S["uk_ready"], 1)
                act.wait_ge(S["kvr"], 3 * j + 3)
                nc.scalar.activation(row["sr"][:], P3[:], ACT.Tanh, scale=0.5).then_inc(S["sr_ready"], 1)
                for n, name in enumerate(("a2", "e2", "a1", "e1")):
                    act.wait_ge(S["logs"], 4 * j + n + 1)
                    nc.scalar.activation(row[name][:], row[name][:], ACT.Exp).then_inc(S["exps"], 1)
                act.wait_ge(S["turned2"], j + 1)
                for r in range(2):
                    nc.scalar.activation(ht[:, 512 * r:512 * r + 512], P1[:, 512 * r:512 * r + 512],
                                         ACT.Identity, bias=w("b2"), scale=w("g2")).then_inc(S["h2_ready"], 1)
                for n in range(8):
                    act.wait_ge(S["up"], 8 * j + n + 1)
                    if n >= 2:
                        wait_past(act, S["kk_ready"], 8 * j + n - 1)
                    bank = (P2, P3)[(n // 2) % 2][:, 512 * (n % 2):512 * (n % 2) + 512]
                    nc.scalar.activation(relu[:, n % 2, :], bank, ACT.Relu).then_inc(S["relu_ready"], 1)
                act.wait_ge(S["gate_psum"], j + 1)
                nc.scalar.activation(th[:], P1[:], ACT.Tanh, scale=0.5).then_inc(S["th_ready"], 1)
            first_then_loop(act, B // 2, each)

        @block.tensor
        def _(pe):
            def half(pair, n):
                return pair[:, 512 * n:512 * n + 512]

            def at(u):
                return 512 * (u % 2) + 128 * (u // 2)

            def each(j):
                pe.wait_ge(S["xn_ready"], 6 * j + 4)
                wait_past(pe, S["kept"], 5 * j)
                for u in range(TT):
                    last = nc.tensor.transpose(P0[:, at(u):at(u) + 128], z[:, u].rearrange("p b c -> p (b c)"),
                                               mem.ident[:])
                last.then_inc(S["turned"], 1)
                pe.wait_ge(S["ht_ready"], 2 * j + 2)
                wait_past(pe, S["th_ready"], j)
                wait_past(pe, S["kk_ready"], 8 * j)
                for pair, name in ((P1, "wk"), (P2, "wv"), (P3, "wr")):
                    for n in range(2):
                        last = nc.tensor.matmul(half(pair, n), w(name), ht[:, 512 * n:512 * n + 512],
                                                start=True, stop=True)
                    last.then_inc(S["kvr"], 1)
                pe.wait_ge(S["sy_ready"], j + 1)
                for u in range(TT):
                    last = nc.tensor.matmul(P0[:, 128 * u:128 * u + 128], row["sy"][:, at(u):at(u) + 128], w("wo"),
                                            start=True, stop=True)
                last.then_inc(S["x1_psum"], 1)
                pe.wait_ge(S["xn_ready"], 6 * j + 6)
                pe.wait_ge(S["uk_ready"], j + 1)
                for u in range(TT):
                    last = nc.tensor.transpose(P1[:, at(u):at(u) + 128], z[:, u].rearrange("p b c -> p (b c)"),
                                               mem.ident[:])
                last.then_inc(S["turned2"], 1)
                pe.wait_ge(S["h2_ready"], 2 * j + 2)
                pe.wait_ge(S["sr_ready"], j + 1)
                for n in range(8):
                    if n >= 4:
                        pe.wait_ge(S["kk_ready"], 8 * j + n - 3)
                    nc.tensor.matmul(half((P2, P3)[(n // 2) % 2], n % 2), w("wkf")[:, 128 * (n // 2):128 * (n // 2) + 128],
                                     ht[:, 512 * (n % 2):512 * (n % 2) + 512], start=True, stop=True
                                     ).then_inc(S["up"], 1)
                for u in range(TT):
                    last = nc.tensor.matmul(P1[:, 128 * u:128 * u + 128], ht[:, at(u):at(u) + 128], w("wrf"),
                                            start=True, stop=True)
                last.then_inc(S["gate_psum"], 1)
                pe.wait_ge(S["kk_ready"], 8 * j + 8)
                for u in range(TT):
                    for c in range(4):
                        last = nc.tensor.matmul(P0[:, 128 * u:128 * u + 128], kk[:, c, at(u):at(u) + 128],
                                                w("wvf")[:, 128 * c:128 * c + 128], start=(c == 0), stop=(c == 3))
                last.then_inc(S["down"], 1)
            first_then_loop(pe, B // 2, each)


def more_images(a, put, both, every):
    wq, wk = a["L2_attn_Wq"].T, a["L2_attn_Wk"].T
    for n, m in enumerate((wq, wq, wk, wk)):
        both("attn2", "wqk", m, C * n)
    both("attn1", "wq", a["L1_attn_Wq"])
    both("attn1", "wkv", a["L1_attn_Wk"])
    both("attn1", "wkv", a["L1_attn_Wv"], C)
    put("attn1", "wm", a["L1_attn_Wm"])
    put("attn1", "w1", a["L1_attn_W1"])
    put("attn1", "w2", a["L1_attn_W2"])
    for n in ("g1", "b1", "g2", "b2"):
        every("attn1", n, a["L1_attn_" + n])
    import numpy as np
    put("attn1", "head", np.kron(np.eye(H1, dtype=np.float32), np.ones((D1, D1), np.float32)))

    def twice(name, m, c0=0):
        m = np.asarray(m)
        put("attn3", name, m, 0, c0)
        put("attn3", name, m, 64, c0 + m.shape[1])

    for name, key in (("wk", "Wk"), ("wv", "Wv"), ("wr", "Wr"), ("wo", "Wo"), ("wrf", "Wr_ffn")):
        twice(name, a["L3_attn_" + key])
    for c in range(4):
        twice("wkf", a["L3_attn_Wk_ffn"][:, C * c:C * c + C], 128 * c)
        twice("wvf", a["L3_attn_Wv_ffn"][C * c:C * c + C], 128 * c)
    for name, key in (("g1", "g1"), ("b1", "b1"), ("g2", "g2"), ("b2", "b2"), ("decay", "spatial_decay"),
                      ("first", "spatial_first")):
        both("attn3", name, np.asarray(a["L3_attn_" + key]).reshape(C, 1))

    def spread(m, width=1):
        out = np.zeros((128, m.shape[1]), np.float32)
        for h in range(H0):
            out[32 * h:32 * h + DH0] = m[DH0 * h:DH0 * h + DH0]
        return out

    both("attn0", "wq", spread(np.asarray(a["L0_attn_Wq"])).T)
    both("attn0", "wk", spread(np.asarray(a["L0_attn_Wk"])).T)
    put("attn0", "wv", a["L0_attn_Wv"].T)
    put("attn0", "wv", a["L0_attn_bv"].reshape(1, C), C)
    put("attn0", "wo", a["L0_attn_Wo"].T)
    put("attn0", "wo", a["L0_attn_bo"].reshape(1, C), C)
    put("attn0", "bq", spread(np.asarray(a["L0_attn_bq"]).reshape(C, 1)))
    put("attn0", "bk", spread(np.asarray(a["L0_attn_bk"]).reshape(C, 1)))
    for h in range(H0):
        put("attn0", "bq", np.full((1, 1), DH0 ** 0.5, np.float32), 32 * h + DH0)
        put("attn0", "right", np.full((1, WINDOW), MASKED, np.float32), 32 * h + DH0)
        put("attn0", "headmask", np.ones((QB, DH0), np.float32), 32 * h, DH0 * h)
        put("attn0", "selq", np.eye(QB, dtype=np.float32), 32 * h)
        put("attn0", "slope", np.broadcast_to(a["L0_attn_alibi_slope"][h], (QB, 1)), 32 * h)
        put("attn0", "shift", np.broadcast_to(a["L0_attn_shift_logits"][h], (QB, 4)), 32 * h)
    every("attn0", "svals", np.asarray(SHIFTS, np.float32))
    ql = np.arange(128)[:, None] % QB
    d = np.arange(SW)[None, :] - SMAX - ql
    near = (d >= -SMAX) & (d < WINDOW)
    put("attn0", "dist", np.where(near, d, 0).astype(np.float32))
    put("attn0", "pen", np.where(near, 0, MASKED).astype(np.float32))
    d = np.arange(KW)[:, None] - np.arange(128)[None, :] % QB
    put("attn0", "keep", ((d >= 0) & (d < WINDOW)).astype(np.float32))


def stage_out(nc, mem, out):
    with ExitStack() as ctx:
        stored = ctx.enter_context(nc.semaphore("stored"))
        block = ctx.enter_context(nc.Block())

        @block.sync
        def _(sp):
            for b in range(B):
                for s in range(2):
                    sp.dma_start(out[b].rearrange("(v k s r) c -> s v k r c", k=4, s=2, r=2)[s],
                                 mem.h[64 * s:64 * s + 64, b, :, :].rearrange("p (k r) c -> p k r c", r=2)
                                 ).then_inc(stored, 16)
            sp.wait_ge(stored, 32 * B)


def program(nc, x, images, out, stages=None, h_in=None):
    with ExitStack() as ctx:
        mem = Memory(nc, ctx)
        mem.images = {n: mem.sb(f"img_{n}", [128, columns(n)[1]]) for n in IMAGES}
        stage_tok(nc, mem, x, images)
        for name in (stages if stages is not None else STAGES):
            {"attn0": stage_attn0, "attn1": stage_attn1, "attn2": stage_attn2, "attn3": stage_attn3}.get(
                name, stage_moe)(nc, mem, name, images)
        stage_out(nc, mem, out)


STAGES = ("attn0", "moe0", "attn1", "moe1", "attn2", "moe2", "attn3", "moe3")


def weight_images(a):
    import numpy as np
    img = {n: np.zeros((128, columns(n)[1]), np.float32) for n in IMAGES}

    def put(image, name, value, r0=0, c0=0):
        at, n = columns(image)[0][name]
        value = np.asarray(value)
        img[image][r0:r0 + value.shape[0], at + c0:at + c0 + value.shape[1]] = value

    def both(image, name, value, c0=0):
        put(image, name, value, 0, c0)
        put(image, name, value, 64, c0)

    def every(image, name, row):
        put(image, name, np.broadcast_to(np.asarray(row).reshape(1, -1), (128, np.asarray(row).size)))

    eye, f, j = np.eye(C, dtype=np.float32), np.arange(NF), np.arange(NF)
    angle = 2 * np.pi * np.outer(f, j) / PATCH
    cos, sin = np.cos(angle) / 4, -np.sin(angle) / 4
    sin[:, 0] = sin[:, NF - 1] = sin[0] = sin[NF - 1] = 0
    put("tok", "wt", a["L0_tok_W"].reshape(C, 2, NF, C).transpose(1, 3, 2, 0).reshape(128, NF * C))
    put("tok", "dft", np.broadcast_to(cos.reshape(1, -1), (64, NF * NF)))
    put("tok", "dft", np.broadcast_to(sin.reshape(1, -1), (64, NF * NF)), 64)
    for half in (0, 64):
        put("tok", "sel_first", eye, half, 0)
        put("tok", "sel_first", eye, half, 128)
    put("tok", "sel_second", eye, 0, 64)
    put("tok", "sel_second", -eye, 64, 64)
    both("moe0", "w1", a["L0_ffn_w1"].transpose(1, 0, 2).reshape(C, E * C))
    for e in range(E):
        put("moe0", "w2", a["L0_ffn_w2"][e], 64 * (e % 2), 128 * (e // 2) + 64 * (e % 2))
        put("moe0", "b1", a["L0_ffn_b1"][e][:, None], 64 * (e % 2), e // 2)
    both("moe0", "wr", a["L0_ffn_router_w"].T)
    put("moe0", "b2", a["L0_ffn_b2"])
    w1 = a["L1_ffn_W1"].transpose(2, 0, 1).reshape(C, E * HID)
    w2 = a["L1_ffn_W2"].transpose(0, 2, 1).reshape(16, 128, C).transpose(1, 0, 2).reshape(128, 16 * C)
    for name, w1, w2, wr, b1, b2, br in (
            ("moe1", w1, w2, a["L1_ffn_Wg"].T, a["L1_ffn_b1"], a["L1_ffn_b2"], a["L1_ffn_bg"]),
            ("moe2", a["L2_ffn_W1"].transpose(1, 0, 2).reshape(C, E * HID),
             a["L2_ffn_W2"].reshape(16, 128, C).transpose(1, 0, 2).reshape(128, 16 * C),
             a["L2_ffn_Wg"], a["L2_ffn_b1"], a["L2_ffn_b2"], a["L2_ffn_bg"])):
        both(name, "w1", w1)
        put(name, "w2", w2)
        both(name, "wr", wr)
        put(name, "b1", b1.reshape(16, 128).T)
        put(name, "b2", b2)
        every(name, "br", br)
    both("moe3", "w1", a["L3_ffn_W1"])
    put("moe3", "b1", a["L3_ffn_b1"].reshape(2, 128).T)
    put("moe3", "wr", a["L3_ffn_Wg"].reshape(2, 128, E).transpose(1, 0, 2).reshape(128, 2 * E))
    put("moe3", "w2", a["L3_ffn_Wd"].reshape(E, 2, 128, C).transpose(2, 1, 0, 3).reshape(128, 2 * E * C))
    put("moe3", "b2", a["L3_ffn_bd"])
    every("moe3", "br", a["L3_ffn_bg"])
    more_images(a, put, both, every)
    img["ident"] = np.eye(128, dtype=np.float32)
    img["iota"] = np.broadcast_to(np.arange(E, dtype=np.float32), (128, TT, E)).reshape(128, TT * E)
    return img


def kernel(**inputs):
    import numpy as _np
    import concourse.bacc as _bacc
    from concourse import mybir as _mybir
    from concourse.bass_utils import run_bass_kernel_spmd as _run

    a = {k: _np.asarray(v) for k, v in inputs.items()}
    arrays = {f"image_{n}": _np.ascontiguousarray(v) for n, v in weight_images(a).items()}
    arrays["x"] = _np.ascontiguousarray(a["x"])
    nc = _bacc.Bacc("TRN2", target_bir_lowering=False, num_devices=1)
    dram = {n: nc.dram_tensor(n, v.shape, _mybir.dt.from_np(v.dtype), kind="ExternalInput").ap()
            for n, v in arrays.items()}
    out = nc.dram_tensor("out", (B, L, C), F32, kind="ExternalOutput").ap()
    program(nc, dram["x"], {n[6:]: v for n, v in dram.items() if n != "x"}, out)
    r = _run(nc, [arrays], core_ids=[0])
    return r.results[0]["out"]
```
